# Optimizing a Trainium2 kernel written in Bass

```python
import numpy as np
import jax
import jax.numpy as jnp

def _softmax(x, axis=-1):
    return jax.nn.softmax(x, axis=axis)

def _gelu(x):
    return jax.nn.gelu(x, approximate=True)

def _silu(x):
    return jax.nn.silu(x)

def _sigmoid(x):
    return jax.nn.sigmoid(x)

def _layernorm(x, axis=-1, eps=1e-05):
    m = jnp.mean(x, axis=axis, keepdims=True)
    v = jnp.var(x, axis=axis, keepdims=True)
    return (x - m) / jnp.sqrt(v + eps)

def _scatter_add(tgt, idx, src, axis=0):
    return tgt.at[idx].add(src)

def _segment_sum(src, seg, n):
    return jax.ops.segment_sum(src, seg, n)
kernel_name = 'mk_early_fusion_d1_tok_img768_r4_bc4e1a'

def setup_inputs(seed: int=0):
    np.random.seed(seed)
    _w = jnp.asarray

    def _rec_inputs():
        import jax
        import jax.numpy as jnp
        _rk = jax.random.key(seed)
        x = -0.000596345 + 1.00056 * jax.random.normal(jax.random.fold_in(_rk, 1), (8, 3, 64, 64), jnp.float32)
        txt = -0.000190561 + 0.886117 * jax.random.normal(jax.random.fold_in(_rk, 2), (8, 128, 192), jnp.float32)
        return (x, txt)
    x, txt = _rec_inputs()

    def _L0_tok_setup():
        import jax, jax.numpy as jnp
        import numpy as np
        B = 16
        IMG = 64
        CH = 3
        EMBED = 64
        GP = 16
        PRE = [1, 2, 4]
        N_LEVELS = 3
        FUSED = EMBED * N_LEVELS

        def hilbert_flat_indices(n):
            t = np.arange(n * n, dtype=np.int64)
            x = np.zeros(n * n, dtype=np.int64)
            y = np.zeros(n * n, dtype=np.int64)
            s = 1
            while s < n:
                rx = 1 & t // 2
                ry = 1 & (t ^ rx)
                swap = ry == 0
                flip = swap & (rx == 1)
                x = np.where(flip, s - 1 - x, x)
                y = np.where(flip, s - 1 - y, y)
                x2 = np.where(swap, y, x)
                y2 = np.where(swap, x, y)
                x, y = (x2, y2)
                x = x + s * rx
                y = y + s * ry
                t = t // 4
                s *= 2
            return y * n + x

        def _level(x, idx, W, b, p, gp):
            Bsz, C, H, _ = x.shape
            h = H // p
            t = x.reshape(Bsz, C, h, p, h, p).transpose(0, 2, 4, 3, 5, 1).reshape(Bsz, h * h, p * p * C)
            t = t[:, idx]
            t = t.reshape(Bsz, h * h // gp, gp * p * p * C)
            return t @ W.T + b

        def _interp_linear(x, n_out):
            L = x.shape[1]
            pos = (jnp.arange(n_out, dtype=jnp.float32) + 0.5) * (L / n_out) - 0.5
            pos = jnp.clip(pos, 0.0, L - 1)
            i0 = jnp.floor(pos).astype(jnp.int32)
            i1 = jnp.minimum(i0 + 1, L - 1)
            w = (pos - i0).astype(x.dtype)
            return x[:, i0] * (1.0 - w)[None, :, None] + x[:, i1] * w[None, :, None]
        key = jax.random.key(seed)
        ks = jax.random.split(key, 9)
        inp = {'x': jax.random.normal(ks[0], (B, CH, IMG, IMG), jnp.float32)}
        for i, p in enumerate(PRE):
            din = CH * p * p * GP
            inp[f'W{i}'] = jax.random.normal(ks[1 + 2 * i], (EMBED, din), jnp.float32) * din ** (-0.5)
            inp[f'b{i}'] = jax.random.normal(ks[2 + 2 * i], (EMBED,), jnp.float32) * 0.02
        inp['Wf'] = jax.random.normal(ks[7], (FUSED, FUSED), jnp.float32) * FUSED ** (-0.5)
        inp['bf'] = jax.random.normal(ks[8], (FUSED,), jnp.float32) * 0.02
        for i, p in enumerate(PRE):
            inp[f'idx{i}'] = jnp.asarray(hilbert_flat_indices(IMG // p), jnp.int32)
        return inp
    _L0_tok_all = _L0_tok_setup()
    _L0_tok_in = {k: v for k, v in _L0_tok_all.items() if k in ('W0', 'b0', 'W1', 'b1', 'W2', 'b2', 'Wf', 'bf', 'idx0', 'idx1', 'idx2')}
    del _L0_tok_all

    def _L0_attn_setup():
        import jax, jax.numpy as jnp
        import numpy as np
        B, S, D, H = (64, 577, 192, 12)
        DH = D // H
        key = jax.random.key(seed)
        ks = jax.random.split(key, 9)
        sc = 0.02
        return {'x': jax.random.normal(ks[0], (B, S, D), jnp.float32), 'Wq': jax.random.normal(ks[1], (H, D, DH), jnp.float32) * sc, 'bq': jnp.zeros((H, DH), jnp.float32), 'Wk': jax.random.normal(ks[2], (H, D, DH), jnp.float32) * sc, 'bk': jnp.zeros((H, DH), jnp.float32), 'Wv': jax.random.normal(ks[3], (H, D, DH), jnp.float32) * sc, 'bv': jnp.zeros((H, DH), jnp.float32), 'Wo': jax.random.normal(ks[4], (D, D), jnp.float32) * sc, 'bo': jnp.zeros((D,), jnp.float32)}
    _L0_attn_all = _L0_attn_setup()
    _L0_attn_in = {k: v for k, v in _L0_attn_all.items() if k in ('Wq', 'bq', 'Wk', 'bk', 'Wv', 'bv', 'Wo', 'bo')}
    del _L0_attn_all

    def _L0_ffn_setup():
        import jax, jax.numpy as jnp
        import numpy as np
        QN, QP = (-8, 7)

        def round_pass(x):
            return x + jax.lax.stop_gradient(jnp.round(x) - x)

        def _quant_act(x, alpha_a):
            a = alpha_a.mean()
            return round_pass(jnp.clip(x / a, QN, QP))

        def _quant_w(w, alpha_w):
            return round_pass(jnp.clip(w / alpha_w[:, None], QN, QP))
        key = jax.random.key(seed)
        ks = jax.random.split(key, 9)
        B, S, D, H = (16, 256, 192, 768)

        def unif(k, shape):
            return jax.random.uniform(k, shape, jnp.float32, 0.02, 0.1)
        return {'x0': jax.random.normal(ks[0], (B, S, D), jnp.float32), 'w1': jax.random.normal(ks[1], (H, D), jnp.float32) * 0.02, 'b1': jax.random.normal(ks[2], (H,), jnp.float32) * 0.02, 'alpha_w1': unif(ks[3], (H,)), 'alpha_a1': unif(ks[4], (D,)), 'w2': jax.random.normal(ks[5], (D, H), jnp.float32) * 0.02, 'b2': jax.random.normal(ks[6], (D,), jnp.float32) * 0.02, 'alpha_w2': unif(ks[7], (D,)), 'alpha_a2': unif(ks[8], (H,))}
    _L0_ffn_all = _L0_ffn_setup()
    _L0_ffn_in = {k: v for k, v in _L0_ffn_all.items() if k in ('w1', 'b1', 'alpha_w1', 'alpha_a1', 'w2', 'b2', 'alpha_w2', 'alpha_a2')}
    del _L0_ffn_all
    return {'x': x, 'txt': txt, 'L0_tok_W0': _L0_tok_in['W0'], 'L0_tok_b0': _L0_tok_in['b0'], 'L0_tok_W1': _L0_tok_in['W1'], 'L0_tok_b1': _L0_tok_in['b1'], 'L0_tok_W2': _L0_tok_in['W2'], 'L0_tok_b2': _L0_tok_in['b2'], 'L0_tok_Wf': _L0_tok_in['Wf'], 'L0_tok_bf': _L0_tok_in['bf'], 'L0_tok_idx0': _L0_tok_in['idx0'], 'L0_tok_idx1': _L0_tok_in['idx1'], 'L0_tok_idx2': _L0_tok_in['idx2'], 'L0_attn_Wq': _L0_attn_in['Wq'], 'L0_attn_bq': _L0_attn_in['bq'], 'L0_attn_Wk': _L0_attn_in['Wk'], 'L0_attn_bk': _L0_attn_in['bk'], 'L0_attn_Wv': _L0_attn_in['Wv'], 'L0_attn_bv': _L0_attn_in['bv'], 'L0_attn_Wo': _L0_attn_in['Wo'], 'L0_attn_bo': _L0_attn_in['bo'], 'L0_ffn_w1': _L0_ffn_in['w1'], 'L0_ffn_b1': _L0_ffn_in['b1'], 'L0_ffn_alpha_w1': _L0_ffn_in['alpha_w1'], 'L0_ffn_alpha_a1': _L0_ffn_in['alpha_a1'], 'L0_ffn_w2': _L0_ffn_in['w2'], 'L0_ffn_b2': _L0_ffn_in['b2'], 'L0_ffn_alpha_w2': _L0_ffn_in['alpha_w2'], 'L0_ffn_alpha_a2': _L0_ffn_in['alpha_a2']}

def reference(x, txt, L0_tok_W0, L0_tok_b0, L0_tok_W1, L0_tok_b1, L0_tok_W2, L0_tok_b2, L0_tok_Wf, L0_tok_bf, L0_tok_idx0, L0_tok_idx1, L0_tok_idx2, L0_attn_Wq, L0_attn_bq, L0_attn_Wk, L0_attn_bk, L0_attn_Wv, L0_attn_bv, L0_attn_Wo, L0_attn_bo, L0_ffn_w1, L0_ffn_b1, L0_ffn_alpha_w1, L0_ffn_alpha_a1, L0_ffn_w2, L0_ffn_b2, L0_ffn_alpha_w2, L0_ffn_alpha_a2):
    import jax
    import jax.numpy as jnp

    def _L0_tok_ref(x, W0, b0, W1, b1, W2, b2, Wf, bf, idx0, idx1, idx2):
        import jax, jax.numpy as jnp
        import numpy as np
        B = 16
        IMG = 64
        CH = 3
        EMBED = 64
        GP = 16
        PRE = [1, 2, 4]
        N_LEVELS = 3
        FUSED = EMBED * N_LEVELS

        def hilbert_flat_indices(n):
            t = np.arange(n * n, dtype=np.int64)
            x = np.zeros(n * n, dtype=np.int64)
            y = np.zeros(n * n, dtype=np.int64)
            s = 1
            while s < n:
                rx = 1 & t // 2
                ry = 1 & (t ^ rx)
                swap = ry == 0
                flip = swap & (rx == 1)
                x = np.where(flip, s - 1 - x, x)
                y = np.where(flip, s - 1 - y, y)
                x2 = np.where(swap, y, x)
                y2 = np.where(swap, x, y)
                x, y = (x2, y2)
                x = x + s * rx
                y = y + s * ry
                t = t // 4
                s *= 2
            return y * n + x

        def _level(x, idx, W, b, p, gp):
            Bsz, C, H, _ = x.shape
            h = H // p
            t = x.reshape(Bsz, C, h, p, h, p).transpose(0, 2, 4, 3, 5, 1).reshape(Bsz, h * h, p * p * C)
            t = t[:, idx]
            t = t.reshape(Bsz, h * h // gp, gp * p * p * C)
            return t @ W.T + b

        def _interp_linear(x, n_out):
            L = x.shape[1]
            pos = (jnp.arange(n_out, dtype=jnp.float32) + 0.5) * (L / n_out) - 0.5
            pos = jnp.clip(pos, 0.0, L - 1)
            i0 = jnp.floor(pos).astype(jnp.int32)
            i1 = jnp.minimum(i0 + 1, L - 1)
            w = (pos - i0).astype(x.dtype)
            return x[:, i0] * (1.0 - w)[None, :, None] + x[:, i1] * w[None, :, None]
        Ws = [(idx0, W0, b0, PRE[0]), (idx1, W1, b1, PRE[1]), (idx2, W2, b2, PRE[2])]
        outs = [_level(x, idx, W, b, p, GP) for idx, W, b, p in Ws]
        n_tokens = outs[0].shape[1]
        outs = [outs[0]] + [_interp_linear(o, n_tokens) for o in outs[1:]]
        y = jnp.concatenate(outs, axis=-1)
        return y @ Wf.T + bf

    def _L0_attn_ref(x, Wq, bq, Wk, bk, Wv, bv, Wo, bo):
        import jax, jax.numpy as jnp
        import numpy as np
        B, S, D, H = (64, 577, 192, 12)
        DH = D // H
        q = jnp.einsum('bsd,hde->bhse', x, Wq) + bq[None, :, None, :]
        k = jnp.einsum('bsd,hde->bhse', x, Wk) + bk[None, :, None, :]
        v = jnp.einsum('bsd,hde->bhse', x, Wv) + bv[None, :, None, :]
        scale = np.float32(1.0 / np.sqrt(DH))
        scores = jnp.einsum('bhqe,bhke->bhqk', q, k) * scale
        probs = jax.nn.softmax(scores, axis=2)
        ctx = jnp.einsum('bhqk,bhke->bhqe', probs, v)
        ctx = ctx.transpose(0, 2, 1, 3).reshape(x.shape[0], x.shape[1], H * DH)
        return ctx @ Wo + bo

    def _L0_ffn_ref(x0, w1, b1, alpha_w1, alpha_a1, w2, b2, alpha_w2, alpha_a2):
        import jax, jax.numpy as jnp
        import numpy as np
        QN, QP = (-8, 7)

        def round_pass(x):
            return x + jax.lax.stop_gradient(jnp.round(x) - x)

        def _quant_act(x, alpha_a):
            a = alpha_a.mean()
            return round_pass(jnp.clip(x / a, QN, QP))

        def _quant_w(w, alpha_w):
            return round_pass(jnp.clip(w / alpha_w[:, None], QN, QP))
        xq = _quant_act(x0, alpha_a1)
        wq1 = _quant_w(w1, alpha_w1)
        x1 = jnp.einsum('bsd,hd->bsh', xq, wq1)
        x1 = x1 * alpha_w1 * alpha_a1.mean() + b1
        x1 = jax.nn.gelu(x1, approximate=False)
        x1 = jnp.clip(x1, -10.0, 10.0)
        hq = _quant_act(x1, alpha_a2)
        wq2 = _quant_w(w2, alpha_w2)
        x2 = jnp.einsum('bsh,dh->bsd', hq, wq2)
        x2 = x2 * alpha_w2 * alpha_a2.mean() + b2
        return x2
    h = _L0_tok_ref(x, L0_tok_W0, L0_tok_b0, L0_tok_W1, L0_tok_b1, L0_tok_W2, L0_tok_b2, L0_tok_Wf, L0_tok_bf, L0_tok_idx0, L0_tok_idx1, L0_tok_idx2)
    h = jnp.concatenate([h, txt], axis=1)
    h = h + _L0_attn_ref(_layernorm(h, axis=-1), L0_attn_Wq, L0_attn_bq, L0_attn_Wk, L0_attn_bk, L0_attn_Wv, L0_attn_bv, L0_attn_Wo, L0_attn_bo)
    h = h + _L0_ffn_ref(_layernorm(h, axis=-1), L0_ffn_w1, L0_ffn_b1, L0_ffn_alpha_w1, L0_ffn_alpha_a1, L0_ffn_w2, L0_ffn_b2, L0_ffn_alpha_w2, L0_ffn_alpha_a2)
    return h

_drawn_inputs = setup_inputs


def setup_inputs(seed=0):
    import zlib

    import numpy as np

    out = dict(_drawn_inputs(seed))
    spreads = {'L0_attn_bq': (0.0, 2.0),
     'L0_attn_bk': (0.0, 0.8),
     'L0_attn_bv': (0.0, 0.1),
     'L0_attn_bo': (0.0, 0.1)}
    factors = {'L0_tok_b0': 5.3,
     'L0_tok_b1': 5.309,
     'L0_tok_b2': 4.733,
     'L0_tok_bf': 2.86,
     'L0_attn_Wq': 8.0,
     'L0_attn_Wk': 8.0,
     'L0_attn_Wv': 4.954,
     'L0_ffn_b1': 4.92,
     'L0_ffn_alpha_a2': 64.0,
     'L0_ffn_alpha_w1': 3.084,
     'L0_ffn_alpha_w2': 3.907}
    for name, (base, spread) in spreads.items():
        noise = np.random.default_rng([zlib.crc32(name.encode()), seed]).standard_normal(out[name].shape)
        drawn = base * np.exp(spread * noise) if base else spread * noise
        out[name] = jnp.asarray(drawn.astype(out[name].dtype))
    for name, factor in factors.items():
        out[name] = (out[name] * factor).astype(out[name].dtype)
    return out
```

```python
from contextlib import ExitStack

import numpy as np

import concourse.bass as bass
from concourse import mybir

F32, BF16, I32 = mybir.dt.float32, mybir.dt.bfloat16, mybir.dt.int32
ALU = mybir.AluOpType
ACT = mybir.ActivationFunctionType
AX = mybir.AxisListType

B, CH, IMG = 8, 3, 64
GP = 16
NTOK, NTXT, D = 256, 128, 192
S = NTOK + NTXT
T = S // 128
EMB = 64
H, DH = 12, 16
HID = 768
MH = HID // 128
DC = D // 2
F0, F1, F2 = CH, 4 * CH, 16 * CH
G1, G2 = 64, 16
R0 = GP * F0
GROUPS, BLOCKS, PAIRS = 3, 9, 18
EPS = 1e-5
ROUND = 1.5 * 2.0 ** 23
QN, QP, CLIP = -8.0, 7.0, 10.0
PARTS_K = (0, 1, 2, 0, 1, 0)
PARTS_Q = (0, 0, 0, 1, 1, 2)
SLOTS = len(PARTS_K)
RUNS = ((0, 3), (3, 2), (5, 1))

PREP = ["turn_patches", "tokens", "turn_x0", "turn_x1", "qk0", "qk1", "qk2", "v01", "v2"]
TAIL = ["out01", "out2", "turn_xq"]
BOTH = ["turn_patches", "tokens", "out01", "out2", "turn_x0", "turn_x1", "qk0", "qk1", "qk2",
        "v01", "v2", "turn_xq"]
SLOT = {"turn_patches": 0, "tokens": 1, "out01": 2, "out2": 3, "turn_x0": 4, "turn_x1": 4,
        "qk0": 5, "qk1": 5, "qk2": 6, "v01": 7, "v2": 7, "turn_xq": 8}


def step_index(step, body):
    if isinstance(body, int) and body < 0:
        return PREP.index(step)
    if isinstance(body, int) and body == 0:
        return len(PREP) + PREP.index(step)
    if isinstance(body, int) and body >= B - 1:
        return 2 * len(PREP) + len(BOTH) * (B - 2) + len(TAIL) * (body - (B - 1)) + TAIL.index(step)
    return (body - 1) * len(BOTH) + (2 * len(PREP) + BOTH.index(step))


def earlier(count, b, p):
    return (b - p) * (count // 2)


def wait(eng, sem, value):
    if not isinstance(value, int) or value > 0:
        eng.wait_ge(sem, value)


def wait_behind(eng, constant, *waits):
    values = [(s, v if isinstance(v, int) else eng.to_reg(v)) for s, v in waits]
    eng.wait_ge(*constant)
    for s, v in values:
        wait(eng, s, v)


def build(nc, a, out):
    ctx = ExitStack()
    with ctx:
        def sb(name, shape, dt=F32):
            return ctx.enter_context(nc.sbuf_tensor(name, shape, dt))

        def sem(name):
            return ctx.enter_context(nc.semaphore(name))

        ident = sb("ident", [128, 128])
        identb = sb("identb", [128, 128], BF16)
        x0i, x1i, x2i = sb("x0i", [128, 2, GP], I32), sb("x1i", [128, 8], I32), sb("x2i", [128, 2], I32)
        rows0 = sb("rows0", [128, 2, GP, B * F0])
        rows1 = sb("rows1", [128, 8, B * F1])
        rows2 = sb("rows2", [128, 2, B * F2])
        wfT = sb("wfT", [EMB, 3, D])
        w0 = sb("w0", [EMB, R0])
        w1T = sb("w1T", [8 * F1, 2, EMB])
        w2T = sb("w2T", [F2, GP, EMB])
        bcol = sb("bcol", [EMB, 3])
        bfrow = sb("bfrow", [1, D])
        ones = sb("ones", [1, 128])
        y1T, y2T = sb("y1T", [EMB, B * G1]), sb("y2T", [EMB, B * G2])
        z1, z2 = sb("z1", [128, B // 2, D]), sb("z2", [128, D])
        fused = sb("fused", [128, B, D])
        patches = sb("patches", [128, 2, 128])
        patchesT = sb("patchesT", [128, NTOK])

        h = sb("h", [128, T, D])
        stats, meanvar, rstd = sb("stats", [128, T, 6]), sb("meanvar", [128, T, 2]), sb("rstd", [128, 2, T])
        negmean = sb("negmean", [128, T])
        minushalf = sb("minushalf", [128, T])
        xn = sb("xn", [128, T, D])
        resid = sb("resid", [128, 2, T, D])
        xT0, xT1 = sb("xT0", [DC, S]), sb("xT1", [DC, S])
        wqk0, wqk1 = sb("wqk0", [DC, 3, 128]), sb("wqk1", [DC, 3, 128])
        wv0, wv1 = sb("wv0", [DC, D]), sb("wv1", [DC, D])
        bqk = sb("bqk", [128, 3])
        qkscale = sb("qkscale", [128, 3])
        bvrow, borow, b2row = sb("bvrow", [128, D]), sb("borow", [128, D]), sb("b2row", [128, D])
        full = sb("full", [128, 2, S])
        rest = sb("rest", [128, 2, S])
        parts = sb("parts", [128, 3, 3, S], BF16)
        stackq = sb("stackq", [SLOTS * DH, 2, H, S], BF16)
        stackk = sb("stackk", [SLOTS * DH, 2, H, S], BF16)
        rows1b = full[:].rearrange("p k n -> p (k n)").rearrange("p (b x) -> p b x", b=B)
        t1T = stackk[:, 1].rearrange("p h n -> p (h n)").bitcast(F32)[:, 0:B * 128].rearrange(
            "p (b t) -> p b t", b=B)
        t2T = stackq[0:F2, 1].rearrange("p h n -> p (h n)").bitcast(F32)[:, 0:2 * B * 128].rearrange(
            "p (j b t) -> p j b t", j=2, b=B)
        v = sb("v", [128, 2, T, D])
        negmax, sums, inv = sb("negmax", [128, 3, 2]), sb("sums", [128, 3, 4]), sb("inv", [128, 3, 4])
        probs = sb("probs", [128, 3, 4, S])
        vs = sb("vs", [128, 3, 4, 32])
        ctxT = sb("ctxT", [128, GROUPS, S])
        wo = sb("wo", [128, GROUPS, D])
        h2 = sb("h2", [128, T, D])
        stats2, meanvar2, rstd2 = sb("stats2", [128, T, 6]), sb("meanvar2", [128, T, 2]), sb("rstd2", [128, 2, T])
        negmean2 = sb("negmean2", [128, T])
        xn2 = sb("xn2", [128, T, D])
        xr = sb("xr", [128, T, D])
        xhi, xq = sb("xhi", [128, T, D], BF16), sb("xq", [128, T, D], BF16)
        resid2 = sb("resid2", [128, B * T, D])
        xqT0, xqT1 = sb("xqT0", [DC, B * S], BF16), sb("xqT1", [DC, B * S], BF16)

        w1f0, w1f1 = sb("w1f0", [DC, HID]), sb("w1f1", [DC, HID])
        w1q0, w1q1 = sb("w1q0", [DC, HID], BF16), sb("w1q1", [DC, HID], BF16)
        w2f = sb("w2f", [128, MH, D])
        w2q = sb("w2q", [128, MH, D], BF16)
        aw1row, aw2row = sb("aw1row", [128, HID]), sb("aw2row", [128, D])
        aa1row, aa2row = sb("aa1row", [128, D]), sb("aa2row", [128, HID])
        aw1col, b1col = sb("aw1col", [128, MH]), sb("b1col", [128, MH])
        mean1, mean2 = sb("mean1", [128, 1]), sb("mean2", [128, 1])
        inv1, inv2 = sb("inv1", [128, 1]), sb("inv2", [128, 1])
        top2, low2 = sb("top2", [128, 1]), sb("low2", [128, 1])
        scale1 = sb("scale1", [128, MH])
        scale2 = sb("scale2", [128, D])
        spare = probs[:].rearrange("p r j n -> p (r j) n")
        act_, rounded = spare[:, 0:3], spare[:, 3:6]
        hhi = sb("hhi", [128, 3, S], BF16)
        hq = sb("hq", [128, 2, MH, S], BF16)
        scaled, result = (spare[:, k:k + 3].rearrange("p r n -> p (r n)").rearrange("p (q t d) -> p q t d", q=2, t=T)
                          for k in (6, 9))

        cut = nc.dram_tensor("cut", (2, 2, 3, DH, H, S), BF16, kind="Internal").ap()

        PS = ctx.enter_context(nc.psum_tensor("PS", [128, 8, 512], F32))
        CTX, MISC = 6, 7
        miscb = PS[:, MISC, :].bitcast(BF16)

        idx_in, consts_in = sem("idx_in"), sem("consts_in")
        tokw_in, attw_in, ffnw_in = sem("tokw_in"), sem("attw_in"), sem("ffnw_in")
        got2, got1, got0 = sem("got2"), sem("got1"), sem("got0")
        pe_set, dve_set = sem("pe_set"), sem("dve_set")
        prep_chain = sem("prep_chain")
        pool_set, pool_chain = sem("pool_set"), sem("pool_chain")
        fused_in, text_in = sem("fused_in"), sem("text_in")
        patches_in = sem("patches_in")
        bank_full, bank_read = sem("bank_full"), sem("bank_read")
        stats_in, meanvar_in, text_used = sem("stats_in"), sem("meanvar_in"), sem("text_used")
        var_in, rstd_in, negmean_in, xn_in = sem("var_in"), sem("rstd_in"), sem("negmean_in"), sem("xn_in")
        part1_in, rest_in, part2_in, part3_in = sem("part1_in"), sem("rest_in"), sem("part2_in"), sem("part3_in")
        cut_in = [sem(f"cut_in{mt}") for mt in range(3)]
        stack_in = [[sem(f"stack_in{p}{half}") for half in range(2)] for p in range(2)]
        scores_in, max_in, exp_in, inv_in, vs_in = (sem("scores_in"), sem("max_in"), sem("exp_in"),
                                                   sem("inv_in"), sem("vs_in"))
        pv_done, ctx_in = sem("pv_done"), sem("ctx_in")
        stats2_in, meanvar2_in = sem("stats2_in"), sem("meanvar2_in")
        var2_in, rstd2_in, negmean2_in, xn2_in = sem("var2_in"), sem("rstd2_in"), sem("negmean2_in"), sem("xn2_in")
        xr_in, xhi_in, xq_in, resid2_in = sem("xr_in"), sem("xhi_in"), sem("xq_in"), sem("resid2_in")
        hid_in, gelu_in, rounded_in, hhi_in, hq_in = (sem("hid_in"), sem("gelu_in"), sem("rounded_in"),
                                                      sem("hhi_in"), sem("hq_in"))
        ffn_in, scaled_in, result_in, stored = sem("ffn_in"), sem("scaled_in"), sem("result_in"), [sem("stored0"), sem("stored1")]

        N_TOKW, N_ATTW, N_FFNW = 8, 11, 9

        block = ctx.enter_context(nc.Block())

        @block.sync
        def _(sp):
            for dst, src in ((x2i, "idx2"), (x1i, "idx1"), (x0i, "idx0")):
                sp.dma_start(dst[:], a[src]).then_inc(idx_in, 16)
            sp.dma_start(ident[:], a["ident"]).then_inc(consts_in, 16)
            sp.dma_start(patches[:, :, R0:128], a["interp"]).then_inc(consts_in, 16)
            for dst, src in ((w2T, "W2T"), (w1T, "W1T"), (w0, "W0"), (wfT, "WfT")):
                sp.dma_start(dst[:], a[src]).then_inc(tokw_in, 16)
            for n in range(3):
                sp.dma_start(bcol[:, n:n + 1], a[f"b{n}"]).then_inc(tokw_in, 16)
            sp.dma_start(bfrow[:], a["bf"]).then_inc(tokw_in, 16)
            sp.dma_start(h[:, 2, :], a["txt"][0]).then_inc(text_in, 16)
            sp.wait_ge(dve_set, Z2_COPIED)
            for b in range(B):
                sp.dma_start(fused[128 - G2:128, b, :], z2[G2 * b:G2 * (b + 1), :]).then_inc(fused_in, 16)
            sp.wait_ge(dve_set, Z1_COPIED)
            f = fused[R0:R0 + G1, :, :].rearrange("p (q r) d -> p r q d", r=2)
            for r in range(2):
                sp.dma_start(f[:, r], z1[G1 * r:G1 * (r + 1), :, :]).then_inc(fused_in, 16)

            def store_parts(c, p, mt):
                wait_behind(sp, (idx_in, 48), (part2_in, 3 * c + mt + 1), (part3_in, 3 * c + mt + 1),
                            (stack_in[p][0 if mt < 2 else 1], earlier(16 * 2 * len(RUNS), c, p)))
                for k, first, n, h0 in (((mt, 0, 8, 0),) if mt < 2 else ((0, 0, 4, 8), (1, 64, 4, 8))):
                    for part in range(3):
                        sp.dma_start(cut[p, k, part, :, h0:h0 + n, :].rearrange("e h n -> h e n"),
                                     parts[first:first + DH * n, mt, part, :]).then_inc(cut_in[mt], 16)

            def load_stacks(c, p, half):
                if half == 0:
                    wait_behind(sp, (idx_in, 48), (scores_in, PAIRS * (c - 1)), (cut_in[0], 16 * 3 * (c + 1)),
                                (cut_in[1], 16 * 3 * (c + 1)))
                else:
                    wait_behind(sp, (idx_in, 48), (scores_in, PAIRS * (c - 1)), (cut_in[2], 16 * 6 * (c + 1)))
                h0, n = ((0, 8), (8, 4))[half]
                for s, k in RUNS:
                    rows = slice(DH * s, DH * (s + k))
                    part = PARTS_Q[s]
                    sp.dma_start(stackq[rows, p, h0:h0 + n, :],
                                 cut[p, 0, part:part + 1, :, h0:h0 + n, :].broadcast_to([k, DH, n, S])).then_inc(stack_in[p][half], 16)
                    sp.dma_start(stackk[rows, p, h0:h0 + n, :], cut[p, 1, 0:k, :, h0:h0 + n, :]).then_inc(stack_in[p][half], 16)

            def stacks(c, p):
                for mt in range(3):
                    store_parts(c, p, mt)
                    if mt > 0:
                        load_stacks(c, p, mt - 1)

            def text(c):
                wait(sp, text_used, c)
                wait(sp, meanvar_in, c)
                sp.dma_start(h[:, 2, :], a["txt"][c]).then_inc(text_in, 16)

            stacks(0, 0)
            text(1)
            stacks(1, 1)
            with sp.Fori(1, B // 2) as i:
                for p in range(2):
                    text(2 * i + p)
                    stacks(2 * i + p, p)

            def store(b, p):
                sp.wait_ge(result_in, b + 1)
                sp.dma_start(out[b], result[:, p]).then_inc(stored[p], 16)

            with sp.Fori(0, B // 2) as i:
                for p in range(2):
                    store(2 * i + p, p)
            for p in range(2):
                sp.wait_ge(stored[p], 16 * (B // 2))

        @block.gpsimd
        def _(pool):
            nc.gpsimd.memset(ones[:], 1.0).then_inc(pool_set, 1)
            nc.gpsimd.memset(minushalf[:], -0.5).then_inc(pool_set, 1)
            nc.gpsimd.memset(vs[:], 0.0).then_inc(pool_set, 1)
            pool.wait_ge(idx_in, 48)

            def gather(dst, table, idx, done):
                nc.gpsimd.indirect_dma_start(dst, None, table, bass.IndirectOffsetOnAxis(ap=idx, axis=0)).then_inc(done, 16)

            for jh in range(2):
                gather(rows2[:, jh, :], a["table2"], x2i[:, jh:jh + 1], got2)
            for j in range(8):
                gather(rows1[:, j, :], a["table1"], x1i[:, j:j + 1], got1)
            for t in range(2):
                for j in range(GP):
                    gather(rows0[:, t, j, :], a["table0"], x0i[:, t, j:j + 1], got0)

            def patch_columns(c):
                wait(pool, meanvar_in, c)
                nc.gpsimd.tensor_copy(
                    patches[:, :, 0:R0].rearrange("p t (j c) -> p t j c", c=F0),
                    rows0[:, :, :, bass.ds(F0 * c, F0)]).then_inc(patches_in, 1)

            def layernorm(c, p):
                wait_behind(pool, (pool_set, 3), (meanvar_in, c + 1))
                nc.gpsimd.tensor_scalar(rstd[:, 0, :], meanvar[:, :, 1], 1.0, EPS, ALU.mult, ALU.add).then_inc(var_in, 1)
                nc.gpsimd.tensor_scalar(negmean[:], meanvar[:, :, 0], -1.0, 0.0, ALU.mult, ALU.add).then_inc(negmean_in, 1)
                pool.wait_ge(var_in, c + 1)
                nc.gpsimd.tensor_tensor(out=rstd[:, 1, :], in0=rstd[:, 0, :], in1=minushalf[:], op=ALU.pow).then_inc(rstd_in, 1)
                wait_behind(pool, (pool_set, 3), (rstd_in, c + 1), (negmean_in, c + 1), (part1_in, 3 * c))
                for t in range(T):
                    nc.gpsimd.tensor_scalar(xn[:, t, :], h[:, t, :], negmean[:, t:t + 1], rstd[:, 1, t:t + 1],
                                            ALU.add, ALU.mult).then_inc(xn_in, 1)

            def residual(c, p):
                wait(pool, stats2_in, T * (c - 1))
                nc.gpsimd.tensor_tensor(out=resid[:, p], in0=h[:], in1=borow[:].unsqueeze(1).broadcast_to([128, T, D]),
                                        op=ALU.add).then_inc(text_used, 1)

            def rest_after_part1(c, mt):
                pool.wait_ge(part1_in, 3 * c + mt + 1)
                k = mt % 2
                nc.gpsimd.tensor_tensor(out=rest[:, k], in0=full[:, k], in1=parts[:, mt, 0], op=ALU.subtract).then_inc(rest_in, 1)

            def part3(c, mt):
                pool.wait_ge(part2_in, 3 * c + mt + 1)
                k = mt % 2
                nc.gpsimd.tensor_tensor(out=parts[:, mt, 2], in0=rest[:, k], in1=parts[:, mt, 1], op=ALU.subtract).then_inc(part3_in, 1)

            def scale_values(b, p, n):
                g, t, r = n // 3, n % 3, n % 3
                pool.wait_ge(inv_in, BLOCKS * b + n + 1)
                nc.gpsimd.tensor_tensor(
                    out=vs[:, r, :, 0:DH], in0=v[:, p, t, 4 * DH * g:4 * DH * (g + 1)].rearrange("p (h e) -> p h e", e=DH),
                    in1=inv[:, r, :].unsqueeze(2).broadcast_to([128, 4, DH]), op=ALU.mult).then_inc(vs_in, 1)

            def layernorm2(b):
                wait_behind(pool, (pool_set, 3), (meanvar2_in, b + 1))
                nc.gpsimd.tensor_scalar(rstd2[:, 0, :], meanvar2[:, :, 1], 1.0, EPS, ALU.mult, ALU.add).then_inc(var2_in, 1)
                nc.gpsimd.tensor_scalar(negmean2[:], meanvar2[:, :, 0], -1.0, 0.0, ALU.mult, ALU.add).then_inc(negmean2_in, 1)
                pool.wait_ge(var2_in, b + 1)
                nc.gpsimd.tensor_tensor(out=rstd2[:, 1, :], in0=rstd2[:, 0, :], in1=minushalf[:], op=ALU.pow).then_inc(rstd2_in, 1)
                wait_behind(pool, (pool_set, 3), (rstd2_in, b + 1), (negmean2_in, b + 1))
                for t in range(T):
                    nc.gpsimd.tensor_scalar(xn2[:, t, :], h2[:, t, :], negmean2[:, t:t + 1], rstd2[:, 1, t:t + 1],
                                            ALU.add, ALU.mult).then_inc(xn2_in, 1)
                wait_behind(pool, (pool_set, 3), (xn2_in, 3 * b + 3))
                nc.gpsimd.tensor_scalar(xr[:], xn2[:], inv1[:], ROUND, ALU.mult, ALU.add).then_inc(xr_in, 1)
                nc.gpsimd.tensor_tensor(out=resid2[:, bass.ds(T * b, T), :], in0=h2[:],
                                        in1=b2row[:].unsqueeze(1).broadcast_to([128, T, D]), op=ALU.add).then_inc(resid2_in, 1)

            pool.wait_ge(got0, 16 * 2 * GP)
            pool.wait_ge(consts_in, 32)
            patch_columns(0)
            pool.wait_ge(attw_in, 16 * N_ATTW)
            layernorm(0, 0)
            residual(0, 0)
            for mt in range(3):
                rest_after_part1(0, mt)
                part3(0, mt)

            def body(b, p, prep=True, tail=True):
                for n in range(BLOCKS):
                    if n > 0:
                        scale_values(b, p, n - 1)
                    elif tail:
                        scale_values(b - 1, 1 - p, BLOCKS - 1)
                    if prep:
                        if n == 0:
                            patch_columns(b + 1)
                        if n == 2:
                            layernorm(b + 1, 1 - p)
                        if n == 4:
                            residual(b + 1, 1 - p)
                        if n in (5, 6, 7):
                            rest_after_part1(b + 1, n - 5)
                            part3(b + 1, n - 5)
                    if tail and n == 5:
                        layernorm2(b - 1)

            pool.wait_ge(dve_set, WEIGHTS_READY)
            body(0, 0, tail=False)
            with pool.Fori(0, (B - 2) // 2) as i:
                body(2 * i + 1, 1)
                body(2 * i + 2, 0)
            body(B - 1, 1, prep=False)
            scale_values(B - 1, 1, BLOCKS - 1)
            layernorm2(B - 1)

            def round_hidden(b, m):
                r = m % 3
                wait_behind(pool, (pool_set, 3), (gelu_in, MH * b + m + 1), (hhi_in, MH * b + m - 2))
                nc.gpsimd.tensor_scalar(rounded[:, r], act_[:, r], inv2[:], ROUND, ALU.mult, ALU.add).then_inc(rounded_in, 1)

            for m in range(MH):
                round_hidden(0, m)
            with pool.Fori(1, B) as i:
                for m in range(MH):
                    round_hidden(i, m)

        @block.scalar
        def _(act):
            for dst, src in ((wqk0, "wqk0"), (wqk1, "wqk1"), (wv0, "wv0"), (wv1, "wv1"), (bqk, "bqk"), (wo, "wo"),
                             (bvrow, "bvrow"), (borow, "borow"), (b2row, "b2row"), (aa1row, "aa1row"), (aa2row, "aa2row")):
                act.dma_start(dst[:], a[src]).then_inc(attw_in, 16)
            for dst, src in ((w1f0, "w1f0"), (w1f1, "w1f1"), (w2f, "w2f"), (aw1row, "aw1row"), (aw2row, "aw2row"),
                             (aw1col, "aw1col"), (b1col, "b1col")):
                act.dma_start(dst[:], a[src]).then_inc(ffnw_in, 16)

            def body(b):
                for n in range(BLOCKS):
                    r = n % 3
                    wait(act, pv_done, BLOCKS * b + n - 2)
                    for k in range(2):
                        q = (2 * n + k) % 3
                        act.wait_ge(max_in, PAIRS * b + 2 * n + k + 1)
                        for j in range(2):
                            done = nc.scalar.activation(probs[:, r, 2 * k + j, :], PS[:, 2 * q + j, 0:S], ACT.Exp,
                                                        bias=negmax[:, q, j:j + 1], accum_out=sums[:, r, 2 * k + j:2 * k + j + 1])
                        done.then_inc(exp_in, 1)

            body(0)
            with act.Fori(1, B) as i:
                body(i)

            def gelu(b, m):
                wait(act, rounded_in, MH * b + m - 2)
                act.wait_ge(hid_in, MH * b + m + 1)
                nc.scalar.activation(act_[:, m % 3], PS[:, m % 3, 0:S], ACT.Gelu, bias=b1col[:, m:m + 1],
                                     scale=scale1[:, m:m + 1]).then_inc(gelu_in, 1)

            for m in range(MH):
                gelu(0, m)
            with act.Fori(1, B) as i:
                for m in range(MH):
                    gelu(i, m)

        @block.vector
        def _(dve):
            chain = [0]

            def link(instruction):
                chain[0] += 1
                instruction.then_inc(prep_chain, 1)
                dve.wait_ge(prep_chain, chain[0])

            dve.wait_ge(consts_in, 32)
            nc.vector.tensor_copy(identb[:], ident[:]).then_inc(dve_set, 1)
            nc.vector.memset(qkscale[:], 1.0).then_inc(prep_chain, 1)
            chain[0] += 1
            dve.wait_ge(prep_chain, 1)
            link(nc.vector.memset(qkscale[:, 0:1], DH ** -0.5))
            link(nc.vector.memset(qkscale[0:64, 2:3], DH ** -0.5))

            for n in range(4):
                dve.wait_ge(pe_set, n + 1)
                nc.vector.tensor_copy(t2T[:, n // 2, 4 * (n % 2):4 * (n % 2) + 4, :],
                                      PS[0:F2, n, :].rearrange("p (b t) -> p b t", b=4)).then_inc(dve_set, 1)
            dve.wait_ge(pe_set, 5)
            dve.wait_ge(tokw_in, 16 * N_TOKW)
            nc.vector.tensor_scalar(y2T[:], PS[0:EMB, 4, 0:B * G2], bcol[:, 2:3], None, ALU.add).then_inc(dve_set, 1)
            dve.wait_ge(pe_set, 6)
            nc.vector.tensor_copy(z2[:], PS[:, 5, 0:D]).then_inc(dve_set, 1)
            dve.wait_ge(pe_set, 7)
            nc.vector.tensor_copy(fused[0:R0, :, :], PS[0:R0, 6, 0:D].unsqueeze(1).broadcast_to([R0, B, D])).then_inc(dve_set, 1)
            dve.wait_ge(got1, 16 * 8)
            nc.vector.tensor_copy(rows1b.rearrange("p b (j f) -> p j b f", j=8),
                                  rows1[:].rearrange("p j (b f) -> p j b f", b=B)).then_inc(dve_set, 1)
            for n in range(2):
                dve.wait_ge(pe_set, 8 + n)
                nc.vector.tensor_copy(t1T[:, 4 * n:4 * n + 4, :],
                                      PS[0:8 * F1, n, :].rearrange("p (b t) -> p b t", b=4)).then_inc(dve_set, 1)
            dve.wait_ge(pe_set, 10)
            nc.vector.tensor_scalar(y1T[:], PS[0:EMB, 2, :], bcol[:, 1:2], None, ALU.add).then_inc(dve_set, 1)
            for n in range(2):
                dve.wait_ge(pe_set, 11 + n)
                nc.vector.tensor_copy(z1[:, 2 * n:2 * n + 2, :],
                                      PS[:, 3 + n, 0:2 * D].rearrange("p (q d) -> p q d", q=2)).then_inc(dve_set, 1)

            dve.wait_ge(attw_in, 16 * N_ATTW)
            dve.wait_ge(ffnw_in, 16 * 7)
            link(nc.vector.tensor_reduce(out=mean1[:], in_=aa1row[:], axis=AX.X, op=ALU.add))
            link(nc.vector.tensor_scalar(mean1[:], mean1[:], 1.0 / D, None, ALU.mult))
            link(nc.vector.tensor_reduce(out=mean2[:], in_=aa2row[:], axis=AX.X, op=ALU.add))
            link(nc.vector.tensor_scalar(mean2[:], mean2[:], 1.0 / HID, None, ALU.mult))
            link(nc.vector.reciprocal(inv1[:], mean1[:]))
            link(nc.vector.reciprocal(inv2[:], mean2[:]))
            link(nc.vector.tensor_scalar(scale1[:], aw1col[:], mean1[:], None, ALU.mult))
            link(nc.vector.tensor_scalar(scale2[:], aw2row[:], mean2[:], None, ALU.mult))
            link(nc.vector.tensor_scalar(top2[:], inv2[:], CLIP, QP, ALU.mult, ALU.min))
            link(nc.vector.tensor_scalar(top2[:], top2[:], ROUND, ROUND, ALU.add, ALU.subtract))
            link(nc.vector.tensor_scalar(low2[:], inv2[:], -CLIP, QN, ALU.mult, ALU.max))
            link(nc.vector.tensor_scalar(low2[:], low2[:], ROUND, ROUND, ALU.add, ALU.subtract))
            link(nc.vector.reciprocal(aw1row[:], aw1row[:]))
            link(nc.vector.reciprocal(aw2row[:], aw2row[:]))
            for w, wq, r in ((w1f0[:], w1q0[:], aw1row[0:DC]), (w1f1[:], w1q1[:], aw1row[0:DC]),
                             (w2f[:], w2q[:], aw2row[:].unsqueeze(1).broadcast_to([128, MH, D]))):
                link(nc.vector.tensor_tensor(out=w, in0=w, in1=r, op=ALU.mult))
                link(nc.vector.tensor_scalar(w, w, QN, QP, ALU.max, ALU.min))
                link(nc.vector.tensor_scalar(wq, w, ROUND, ROUND, ALU.add, ALU.subtract))
            nc.vector.memset(h2[:, 0, 0:1], 0.0).then_inc(dve_set, 1)

            def full_bank(step, body):
                dve.wait_ge(bank_full, step_index(step, body) + 1)

            def read_patches(c, p, body):
                full_bank("turn_patches", body)
                nc.vector.tensor_copy(patchesT[:], PS[:, MISC, 0:NTOK]).then_inc(bank_read, 1)

            def read_tokens(c, p, body):
                full_bank("tokens", body)
                wait(dve, text_used, c)
                nc.vector.tensor_copy(h[:, 0:2, :], PS[:, MISC, 0:2 * D].rearrange("p (t d) -> p t d", t=2)).then_inc(bank_read, 1)

            def token_stats(c, body):
                dve.wait_ge(bank_read, step_index("tokens", body) + 1)
                dve.wait_ge(text_in, 16 * c + 16)
                for t in range(T):
                    nc.vector.bn_stats(stats[:, t, :], h[:, t, :]).then_inc(stats_in, 1)

            def token_stats_ready(c):
                dve.wait_ge(stats_in, T * c + T)

            def token_meanvar(c):
                for t in range(T):
                    done = nc.vector.bn_aggr(meanvar[:, t, :], stats[:, t, :])
                done.then_inc(meanvar_in, 1)

            def read_x0(c, p, body):
                full_bank("turn_x0", body)
                nc.vector.tensor_copy(xT0[:], PS[0:DC, MISC, 0:S]).then_inc(bank_read, 1)

            def read_x1(c, p, body):
                full_bank("turn_x1", body)
                nc.vector.tensor_copy(xT1[:], PS[0:DC, MISC, 0:S]).then_inc(bank_read, 1)

            def read_qk(c, mt, body):
                full_bank(f"qk{mt}", body)
                k = mt % 2
                wait(dve, rest_in, 3 * c + (0, -1, 1)[mt])
                nc.vector.tensor_scalar(full[:, k], PS[:, MISC, 0:S], bqk[:, mt:mt + 1], qkscale[:, mt:mt + 1],
                                        ALU.add, ALU.mult).then_inc(bank_read, 1)

            def part1(c, mt, body):
                dve.wait_ge(bank_read, step_index(f"qk{mt}", body) + 1)
                wait(dve, cut_in[mt], 16 * 3 * (2 if mt == 2 else 1) * c)
                nc.vector.tensor_copy(parts[:, mt, 0], full[:, mt % 2]).then_inc(part1_in, 1)

            def part2(c, mt):
                dve.wait_ge(rest_in, 3 * c + mt + 1)
                nc.vector.tensor_copy(parts[:, mt, 1], rest[:, mt % 2]).then_inc(part2_in, 1)

            def read_v(c, p, step, body):
                full_bank(step, body)
                wait(dve, vs_in, BLOCKS * (c - 1))
                t, n = (0, 2) if step == "v01" else (2, 1)
                nc.vector.tensor_tensor(out=v[:, p, t:t + n, :], in0=PS[:, MISC, 0:n * D].rearrange("p (t d) -> p t d", t=n),
                                        in1=bvrow[:].unsqueeze(1).broadcast_to([128, n, D]), op=ALU.add).then_inc(bank_read, 1)

            def negative_max(b, n):
                q = n % 3
                dve.wait_ge(scores_in, PAIRS * b + n + 1)
                nc.vector.tensor_reduce(out=negmax[:, q, :], in_=PS[:, 2 * q:2 * q + 2, 0:S], axis=AX.X, op=ALU.max,
                                        negate=True).then_inc(max_in, 1)

            def inverse_sums(b, n):
                dve.wait_ge(exp_in, PAIRS * b + 2 * n + 2)
                nc.vector.reciprocal(inv[:, n % 3, :], sums[:, n % 3, :]).then_inc(inv_in, 1)

            def read_context(b, g):
                dve.wait_ge(pv_done, BLOCKS * b + 3 * g + 3)
                nc.vector.tensor_copy(ctxT[:, g, :], PS[:, CTX, 0:S]).then_inc(ctx_in, 1)

            def read_out(b, p, step, body):
                full_bank(step, body)
                wait(dve, resid2_in, b)
                t, n = (0, 2) if step == "out01" else (2, 1)
                nc.vector.tensor_tensor(out=h2[:, t:t + n, :], in0=PS[:, MISC, 0:n * D].rearrange("p (t d) -> p t d", t=n),
                                        in1=resid[:, p, t:t + n, :], op=ALU.add).then_inc(bank_read, 1)

            def out_stats(b, body):
                dve.wait_ge(bank_read, step_index("out2", body) + 1)
                for t in range(T):
                    nc.vector.bn_stats(stats2[:, t, :], h2[:, t, :]).then_inc(stats2_in, 1)

            def out_stats_ready(b):
                dve.wait_ge(stats2_in, T * b + T)

            def out_meanvar(b):
                for t in range(T):
                    done = nc.vector.bn_aggr(meanvar2[:, t, :], stats2[:, t, :])
                done.then_inc(meanvar2_in, 1)

            def quantise(b):
                dve.wait_ge(xr_in, b + 1)
                nc.vector.tensor_scalar(xhi[:], xr[:], ROUND, QP, ALU.subtract, ALU.min).then_inc(xhi_in, 1)
                dve.wait_ge(xhi_in, b + 1)
                nc.vector.tensor_scalar(xq[:], xhi[:], QN, None, ALU.max).then_inc(xq_in, 1)

            def read_xq(b, body):
                full_bank("turn_xq", body)
                nc.vector.tensor_copy(xqT0[:, bass.ds(S * b, S)], miscb[0:DC, 0:S])
                nc.vector.tensor_copy(xqT1[:, bass.ds(S * b, S)], miscb[0:DC, 512:512 + S]).then_inc(bank_read, 1)

            read_patches(0, 0, -1)
            read_tokens(0, 0, -1)
            token_stats(0, -1)
            token_stats_ready(0)
            token_meanvar(0)
            read_x0(0, 0, -1)
            read_x1(0, 0, -1)
            for mt in range(3):
                read_qk(0, mt, -1)
                part1(0, mt, -1)
                part2(0, mt)
            read_v(0, 0, "v01", -1)
            read_v(0, 0, "v2", -1)

            def body(b, p, prep=True, tail=True):
                c, o, q = b + 1, b - 1, 1 - p
                for n in range(BLOCKS):
                    if n == 2 and prep:
                        token_stats_ready(c)
                    if n == 4 and tail:
                        out_stats_ready(o)
                    negative_max(b, 2 * n)
                    if n == 2 and prep:
                        token_meanvar(c)
                    if n == 4 and tail:
                        out_meanvar(o)
                    negative_max(b, 2 * n + 1)
                    if n > 0:
                        inverse_sums(b, n - 1)
                    elif tail:
                        inverse_sums(o, BLOCKS - 1)
                    if tail and n == 1:
                        read_context(o, 2)
                    if n in (4, 7):
                        read_context(b, (n - 4) // 3)
                    if n == 0 and prep:
                        read_patches(c, q, b)
                    if n == 1 and prep:
                        read_tokens(c, q, b)
                        token_stats(c, b)
                    if n == 2 and tail:
                        read_out(o, q, "out01", b)
                    if n == 3 and tail:
                        read_out(o, q, "out2", b)
                        out_stats(o, b)
                    if n == 7 and tail:
                        quantise(o)
                    if n == 4 and prep:
                        read_x0(c, q, b)
                        read_x1(c, q, b)
                    if n == 5 and prep:
                        read_qk(c, 0, b)
                        part1(c, 0, b)
                        read_qk(c, 1, b)
                        part1(c, 1, b)
                    if n == 6 and prep:
                        part2(c, 0)
                        part2(c, 1)
                        read_qk(c, 2, b)
                        part1(c, 2, b)
                    if n == 7 and prep:
                        part2(c, 2)
                        read_v(c, q, "v01", b)
                        read_v(c, q, "v2", b)
                    if n == 8 and tail:
                        read_xq(o, b)

            body(0, 0, tail=False)
            with dve.Fori(0, (B - 2) // 2) as i:
                body(2 * i + 1, 1)
                body(2 * i + 2, 0)
            body(B - 1, 1, prep=False)
            inverse_sums(B - 1, BLOCKS - 1)
            read_context(B - 1, 2)
            read_out(B - 1, 1, "out01", B)
            read_out(B - 1, 1, "out2", B)
            out_stats(B - 1, B)
            out_stats_ready(B - 1)
            out_meanvar(B - 1)
            quantise(B - 1)
            read_xq(B - 1, B)

            def clip_hidden(b, p, m):
                r = m % 3
                dve.wait_ge(rounded_in, MH * b + m + 1)
                nc.vector.tensor_scalar(hhi[:, r], rounded[:, r], ROUND, top2[:], ALU.subtract, ALU.min).then_inc(hhi_in, 1)
                wait(dve, ffn_in, 2 * (b - 1))
                dve.wait_ge(hhi_in, MH * b + m + 1)
                nc.vector.tensor_scalar(hq[:, p, m], hhi[:, r], low2[:], None, ALU.max).then_inc(hq_in, 1)

            def finish(b, p):
                for k, (t, n) in enumerate(((0, 2), (2, 1))):
                    dve.wait_ge(ffn_in, 2 * b + k + 1)
                    nc.vector.tensor_tensor(
                        out=scaled[:, p, t:t + n, :], in0=PS[:, 4 + 2 * p + k, 0:n * D].rearrange("p (t d) -> p t d", t=n),
                        in1=scale2[:].unsqueeze(1).broadcast_to([128, n, D]), op=ALU.mult).then_inc(scaled_in, 1)
                dve.wait_ge(scaled_in, 2 * b + 2)
                dve.wait_ge(resid2_in, b + 1)
                wait(dve, stored[p], earlier(16, b, p))
                nc.vector.tensor_tensor(out=result[:, p], in0=scaled[:, p], in1=resid2[:, bass.ds(T * b, T), :],
                                        op=ALU.add).then_inc(result_in, 1)

            def ffn(b, p, last=True):
                for m in range(MH):
                    clip_hidden(b, p, m)
                    if last and m == 3:
                        finish(b - 1, 1 - p)

            ffn(0, 0, last=False)
            ffn(1, 1)
            ffn(2, 0)
            with dve.Fori(1, B // 2 - 1) as i:
                ffn(2 * i + 1, 1)
                ffn(2 * i + 2, 0)
            ffn(B - 1, 1)
            finish(B - 1, 1)

        @block.tensor
        def _(pe):
            mm = nc.tensor.matmul
            pe.wait_ge(consts_in, 32)
            pe.wait_ge(got2, 32)
            for n in range(4):
                for k in range(4):
                    jh, b = n // 2, 4 * (n % 2) + k
                    done = nc.tensor.transpose(PS[0:F2, n, 128 * k:128 * (k + 1)], rows2[:, jh, F2 * b:F2 * (b + 1)], ident[:])
                done.then_inc(pe_set, 1)
            pe.wait_ge(tokw_in, 16 * N_TOKW)
            pe.wait_ge(dve_set, 5)
            for j in range(GP):
                jh, jl = j // 8, j % 8
                done = mm(PS[0:EMB, 4, 0:B * G2], w2T[:, j, :], t2T[:, jh, :, G2 * jl:G2 * (jl + 1)], start=(j == 0), stop=(j == GP - 1))
            done.then_inc(pe_set, 1)
            pe.wait_ge(dve_set, 6)
            pe.wait_ge(pool_set, 3)
            mm(PS[:, 5, 0:D], y2T[:], wfT[:, 2, :], start=True, stop=False)
            mm(PS[:, 5, 0:D], bcol[:, 0:1].broadcast_to([EMB, 128]), wfT[:, 0, :], start=False, stop=False)
            mm(PS[:, 5, 0:D], ones[:], bfrow[:], start=False, stop=True).then_inc(pe_set, 1)
            mm(PS[0:R0, 6, 0:D], w0[:], wfT[:, 0, :], start=True, stop=True).then_inc(pe_set, 1)
            pe.wait_ge(dve_set, 9)
            for n in range(2):
                for k in range(4):
                    b = 4 * n + k
                    done = nc.tensor.transpose(PS[0:8 * F1, n, 128 * k:128 * (k + 1)], rows1b[:, b, :], ident[:])
                done.then_inc(pe_set, 1)
            pe.wait_ge(dve_set, 11)
            for jh in range(2):
                done = mm(PS[0:EMB, 2, :], w1T[:, jh, :], t1T[:, :, G1 * jh:G1 * (jh + 1)], start=(jh == 0), stop=(jh == 1))
            done.then_inc(pe_set, 1)
            pe.wait_ge(dve_set, 12)
            for n in range(2):
                for k in range(2):
                    q = 2 * n + k
                    done = mm(PS[:, 3 + n, D * k:D * (k + 1)], y1T[:, 128 * q:128 * (q + 1)], wfT[:, 1, :], start=True, stop=True)
                done.then_inc(pe_set, 1)
            pe.wait_ge(attw_in, 16 * N_ATTW)

            def bank_free(step, body):
                wait(pe, bank_read, step_index(step, body))

            def turn_patches(c, p, body):
                bank_free("turn_patches", body)
                pe.wait_ge(patches_in, c + 1)
                for t in range(2):
                    done = nc.tensor.transpose(PS[:, MISC, 128 * t:128 * (t + 1)], patches[:, t, :], ident[:])
                done.then_inc(bank_full, 1)

            def tokens(c, p, body):
                bank_free("tokens", body)
                for t in range(2):
                    done = mm(PS[:, MISC, D * t:D * (t + 1)], patchesT[:, 128 * t:128 * (t + 1)],
                              fused[:, bass.ds(c, 1), :].rearrange("p o d -> p (o d)"), start=True, stop=True)
                done.then_inc(bank_full, 1)

            def turn_x(c, p, body, part):
                bank_free(f"turn_x{part}", body)
                pe.wait_ge(xn_in, T * c + T)
                for t in range(T):
                    done = nc.tensor.transpose(PS[0:DC, MISC, 128 * t:128 * (t + 1)], xn[:, t, DC * part:DC * (part + 1)], ident[:])
                done.then_inc(bank_full, 1)

            def qk(c, p, body, mt):
                bank_free(f"qk{mt}", body)
                mm(PS[:, MISC, 0:S], wqk0[:, mt, :], xT0[:], start=True, stop=False)
                mm(PS[:, MISC, 0:S], wqk1[:, mt, :], xT1[:], start=False, stop=True).then_inc(bank_full, 1)

            def values(c, p, body, tiles, step):
                bank_free(step, body)
                for k, t in enumerate(tiles):
                    mm(PS[:, MISC, D * k:D * (k + 1)], xT0[:, 128 * t:128 * (t + 1)], wv0[:], start=True, stop=False)
                    done = mm(PS[:, MISC, D * k:D * (k + 1)], xT1[:, 128 * t:128 * (t + 1)], wv1[:], start=False, stop=True)
                done.then_inc(bank_full, 1)

            def project_out(b, body, tiles, step):
                bank_free(step, body)
                pe.wait_ge(ctx_in, GROUPS * b + GROUPS)
                for k, t in enumerate(tiles):
                    for g in range(GROUPS):
                        done = mm(PS[:, MISC, D * k:D * (k + 1)], ctxT[:, g, 128 * t:128 * (t + 1)], wo[:, g, :],
                                  start=(g == 0), stop=(g == GROUPS - 1))
                done.then_inc(bank_full, 1)

            def turn_xq(b, body):
                bank_free("turn_xq", body)
                pe.wait_ge(xq_in, b + 1)
                for t in range(T):
                    nc.tensor.transpose(miscb[0:DC, 128 * t:128 * (t + 1)], xq[:, t, 0:DC], identb[:])
                for t in range(T):
                    done = nc.tensor.transpose(miscb[0:DC, 512 + 128 * t:512 + 128 * (t + 1)], xq[:, t, DC:D], identb[:])
                done.then_inc(bank_full, 1)

            def run(step, b, p, body):
                if step == "turn_patches":
                    turn_patches(b, p, body)
                elif step == "tokens":
                    tokens(b, p, body)
                elif step in ("turn_x0", "turn_x1"):
                    turn_x(b, p, body, int(step[-1]))
                elif step in ("qk0", "qk1", "qk2"):
                    qk(b, p, body, int(step[-1]))
                elif step in ("v01", "v2"):
                    values(b, p, body, (0, 1) if step == "v01" else (2,), step)
                elif step in ("out01", "out2"):
                    project_out(b, body, (0, 1) if step == "out01" else (2,), step)
                else:
                    turn_xq(b, body)

            def scores(b, p, n):
                g, t, k = n // 6, (n % 6) // 2, n % 2
                q = n % 3
                if n % 6 == 0:
                    if g != 1:
                        pe.wait_ge(stack_in[p][g // 2], earlier(16 * 2 * len(RUNS), b, p) + 16 * 2 * len(RUNS))
                wait(pe, exp_in, PAIRS * b + n - 2)
                for j in range(2):
                    head = 4 * g + 2 * k + j
                    done = mm(PS[:, 2 * q + j, 0:S], stackk[:, p, head, 128 * t:128 * (t + 1)], stackq[:, p, head, :],
                              start=True, stop=True)
                done.then_inc(scores_in, 1)

            def context(b, n):
                g, t, r = n // 3, n % 3, n % 3
                pe.wait_ge(vs_in, BLOCKS * b + n + 1)
                if t == 0:
                    wait(pe, ctx_in, GROUPS * b + g)
                for j in range(4):
                    done = mm(PS[32 * j:32 * (j + 1), CTX, 0:S], vs[:, r, j, :], probs[:, r, j, :], start=(t == 0), stop=(t == 2))
                done.then_inc(pv_done, 1)

            for step in PREP:
                if step == "tokens":
                    pe.wait_ge(fused_in, 16 * (B + 2))
                    pe.wait_ge(dve_set, 8)
                run(step, 0, 0, -1)

            def body(b, p, prep=True, tail=True):
                for n in range(BLOCKS):
                    scores(b, p, 2 * n)
                    scores(b, p, 2 * n + 1)
                    if n >= 2:
                        context(b, n - 2)
                    elif tail:
                        context(b - 1, BLOCKS - 2 + n)
                    for step in (BOTH if prep and tail else PREP if prep else TAIL):
                        if SLOT[step] == n:
                            if step in PREP:
                                run(step, b + 1, 1 - p, b)
                            else:
                                run(step, b - 1, 1 - p, b)

            body(0, 0, tail=False)
            with pe.Fori(0, (B - 2) // 2) as i:
                body(2 * i + 1, 1)
                body(2 * i + 2, 0)
            body(B - 1, 1, prep=False)
            for n in (BLOCKS - 2, BLOCKS - 1):
                context(B - 1, n)
            for step in TAIL:
                run(step, B - 1, 1, B)

            def hidden(b, m):
                wait(pe, gelu_in, MH * b + m - 2)
                mm(PS[:, m % 3, 0:S], w1q0[:, 128 * m:128 * (m + 1)], xqT0[:, bass.ds(S * b, S)], start=True, stop=False)
                mm(PS[:, m % 3, 0:S], w1q1[:, 128 * m:128 * (m + 1)], xqT1[:, bass.ds(S * b, S)], start=False, stop=True).then_inc(hid_in, 1)

            def back(b, p):
                pe.wait_ge(hq_in, MH * b + MH)
                for k, tiles in enumerate(((0, 1), (2,))):
                    for i, t in enumerate(tiles):
                        for m in range(MH):
                            done = mm(PS[:, 4 + 2 * p + k, D * i:D * (i + 1)], hq[:, p, m, 128 * t:128 * (t + 1)], w2q[:, m, :],
                                      start=(m == 0), stop=(m == MH - 1))
                    done.then_inc(ffn_in, 1)

            pe.wait_ge(bank_read, step_index("turn_xq", B) + 1)
            pe.wait_ge(dve_set, WEIGHTS_READY)
            for m in range(MH):
                hidden(0, m)

            def ffn(b, p):
                for m in range(MH):
                    hidden(b, m)
                    if m == 2:
                        back(b - 1, 1 - p)

            ffn(1, 1)
            with pe.Fori(1, B // 2) as i:
                ffn(2 * i, 0)
                ffn(2 * i + 1, 1)
            back(B - 1, 1)


Z2_COPIED, Z1_COPIED, WEIGHTS_READY = 7, 14, 15


def interpolation(n_in, n_out):
    pos = np.clip((np.arange(n_out, dtype=np.float32) + 0.5) * (n_in / n_out) - 0.5, 0.0, n_in - 1)
    i0 = np.floor(pos).astype(np.int32)
    i1 = np.minimum(i0 + 1, n_in - 1)
    w = (pos - i0).astype(np.float32)
    m = np.zeros((n_out, n_in), np.float32)
    m[np.arange(n_out), i0] += 1.0 - w
    m[np.arange(n_out), i1] += w
    return m


def kernel(**inputs):
    import concourse.bacc as bacc
    from concourse.bass_utils import run_bass_kernel_spmd

    i = {k: np.asarray(v) for k, v in inputs.items()}
    tok = {k[len("L0_tok_"):]: v for k, v in i.items() if k.startswith("L0_tok_")}
    att = {k[len("L0_attn_"):]: v for k, v in i.items() if k.startswith("L0_attn_")}
    ffn = {k[len("L0_ffn_"):]: v for k, v in i.items() if k.startswith("L0_ffn_")}
    x = i["x"]

    def table(p):
        n = IMG // p
        t = x.reshape(B, CH, n, p, n, p).transpose(2, 4, 0, 3, 5, 1)
        return t.reshape(n * n, B * p * p * CH)

    def heads_first(w):
        return w.transpose(1, 0, 2).reshape(D, H * DH)

    def rows(r):
        return np.broadcast_to(r.reshape(1, -1), (128, r.size))

    wq, wk, wv = (heads_first(att[k]) for k in ("Wq", "Wk", "Wv"))
    bq, bk = att["bq"].reshape(-1), att["bk"].reshape(-1)
    wqk = np.stack([wq[:, :128], wk[:, :128], np.concatenate([wq[:, 128:], wk[:, 128:]], 1)], 1)
    bqk = np.stack([bq[:128], bk[:128], np.concatenate([bq[128:], bk[128:]])], 1)
    wo = np.zeros((4, 32, GROUPS, D), np.float32)
    wo[:, :DH] = att["Wo"].reshape(GROUPS, 4, DH, D).transpose(1, 2, 0, 3)
    arrays = {
        "idx0": tok["idx0"].reshape(2, 128, GP).transpose(1, 0, 2),
        "idx1": tok["idx1"].reshape(G1, 2, 8).transpose(1, 0, 2).reshape(128, 8),
        "idx2": tok["idx2"].reshape(G2, 2, 8).transpose(2, 0, 1).reshape(128, 2),
        "table0": table(1), "table1": table(2), "table2": table(4),
        "ident": np.eye(128, dtype=np.float32),
        "interp": np.concatenate([interpolation(G1, NTOK), interpolation(G2, NTOK)], 1).reshape(2, 128, G1 + G2).transpose(1, 0, 2),
        "W0": tok["W0"],
        "W1T": tok["W1"].T.reshape(2, 8 * F1, EMB).transpose(1, 0, 2),
        "W2T": tok["W2"].T.reshape(GP, F2, EMB).transpose(1, 0, 2),
        "WfT": tok["Wf"].T.reshape(3, EMB, D).transpose(1, 0, 2),
        "b0": tok["b0"].reshape(EMB, 1), "b1": tok["b1"].reshape(EMB, 1), "b2": tok["b2"].reshape(EMB, 1),
        "bf": tok["bf"].reshape(1, D),
        "txt": i["txt"],
        "wqk0": wqk[:DC], "wqk1": wqk[DC:], "wv0": wv[:DC], "wv1": wv[DC:], "bqk": bqk,
        "wo": wo.reshape(128, GROUPS, D),
        "bvrow": rows(att["bv"]), "borow": rows(att["bo"]), "b2row": rows(ffn["b2"]),
        "aa1row": rows(ffn["alpha_a1"]), "aa2row": rows(ffn["alpha_a2"]),
        "w1f0": ffn["w1"].T[:DC], "w1f1": ffn["w1"].T[DC:],
        "w2f": ffn["w2"].T.reshape(MH, 128, D).transpose(1, 0, 2),
        "aw1row": rows(ffn["alpha_w1"]), "aw2row": rows(ffn["alpha_w2"]),
        "aw1col": ffn["alpha_w1"].reshape(MH, 128).T, "b1col": ffn["b1"].reshape(MH, 128).T,
    }
    arrays = {k: np.ascontiguousarray(v) for k, v in arrays.items()}
    nc = bacc.Bacc("TRN2", target_bir_lowering=False, num_devices=1)
    given = {k: nc.dram_tensor(f"in_{k}", v.shape, mybir.dt.from_np(v.dtype), kind="ExternalInput").ap() for k, v in arrays.items()}
    out = nc.dram_tensor("out", (B, S, D), F32, kind="ExternalOutput").ap()
    build(nc, given, out.rearrange("b (t p) d -> b p t d", p=128))
    r = run_bass_kernel_spmd(nc, [{f"in_{k}": v for k, v in arrays.items()}], core_ids=[0])
    return r.results[0]["out"]
```

```python
from contextlib import ExitStack

import numpy as np

import concourse.bass as bass
from concourse import mybir

F32, BF16, I32 = mybir.dt.float32, mybir.dt.bfloat16, mybir.dt.int32
ALU = mybir.AluOpType
ACT = mybir.ActivationFunctionType
AX = mybir.AxisListType

B, CH, IMG = 8, 3, 64
GP = 16
NTOK, NTXT, D = 256, 128, 192
S = NTOK + NTXT
T = S // 128
EMB = 64
H, DH = 12, 16
HID = 768
MH = HID // 128
DC = D // 2
F0, F1, F2 = CH, 4 * CH, 16 * CH
G1, G2 = 64, 16
R0 = GP * F0
GROUPS, BLOCKS, PAIRS = 3, 9, 18
EPS = 1e-5
ROUND = 1.5 * 2.0 ** 23
QN, QP, CLIP = -8.0, 7.0, 10.0
PARTS_K = (0, 1, 2, 0, 1, 0)
PARTS_Q = (0, 0, 0, 1, 1, 2)
SLOTS = len(PARTS_K)
RUNS = ((0, 3), (3, 2), (5, 1))

FRONT = ["turn_patches", "tokens"]
BACK = ["turn_x0", "turn_x1", "qk0", "qk1", "qk2", "v01", "v2"]
TAIL = ["out01", "out2", "turn_xq"]
ALL = ["turn_x0", "out01", "turn_x1", "out2", "qk0", "qk1", "qk2", "v01", "v2", "turn_patches", "tokens",
       "turn_xq"]
BY_SCALAR = ("tokens", "turn_x0", "turn_x1")
ON_TENSOR = {"turn_x0": 3, "out01": 5, "turn_x1": 5, "out2": 6, "qk0": 7, "qk1": 8, "qk2": 9, "v01": 11,
             "v2": 12, "turn_patches": 14, "tokens": 15, "turn_xq": 17}
ON_VECTOR = {"out01": 4, "out2": 6, "out_meanvar": 8, "qk0": 7, "qk1": 8, "qk2": 9, "part20": 8,
             "part21": 9, "part22": 10, "v01": 10, "v2": 12, "turn_patches": 14, "quantise": 15,
             "turn_xq": 17, "token_stats": 15, "token_meanvar": 17}
ON_SCALAR = {"turn_x0": 2, "turn_x1": 3, "tokens": 13, "context": 8}
ON_GPSIMD = {"layernorm": 1, "residual": 8, "rest0": 7, "rest1": 9, "part30": 9, "rest2": 10,
             "part31": 11, "part32": 11, "patches": 10, "layernorm2": 13, "residual2": 16}
INV_LAG, VALUES_LAG, CONTEXT_LAG = 3, 5, 5


def steps_of(body):
    if body == -2:
        return FRONT + BACK
    return [s for s in ALL if (s in TAIL and body >= 1) or (s in BACK and 0 <= body <= B - 2)
            or (s in FRONT and body <= B - 3)]


def steps_before(step, body, among=ALL):
    def count(steps):
        return sum(s in among for s in steps)
    if isinstance(body, int):
        steps = steps_of(body)
        return sum(count(steps_of(n)) for n in range(-2, body)) + count(steps[:steps.index(step)])
    first = sum(count(steps_of(n)) for n in range(-2, 1)) + count(ALL[:ALL.index(step)])
    return (body - 1) * count(ALL) + first


def same_reader(step):
    return [s for s in ALL if (s in BY_SCALAR) == (step in BY_SCALAR)]


def earlier(count, b, p):
    return (b - p) * (count // 2)


def wait(eng, sem, value):
    if not isinstance(value, int) or value > 0:
        eng.wait_ge(sem, value)


def wait_behind(eng, constant, *waits):
    values = [(s, v if isinstance(v, int) else eng.to_reg(v)) for s, v in waits]
    eng.wait_ge(*constant)
    for s, v in values:
        wait(eng, s, v)


def build(nc, a, out):
    ctx = ExitStack()
    with ctx:
        def sb(name, shape, dt=F32):
            return ctx.enter_context(nc.sbuf_tensor(name, shape, dt))

        def sem(name):
            return ctx.enter_context(nc.semaphore(name))

        ident = sb("ident", [128, 128])
        identb = sb("identb", [128, 128], BF16)
        x0i, x1i, x2i = sb("x0i", [128, 2, GP], I32), sb("x1i", [128, 8], I32), sb("x2i", [128, 2], I32)
        rows0 = sb("rows0", [128, 2, GP, B * F0])
        rows1 = sb("rows1", [128, 8, B * F1])
        rows2 = sb("rows2", [128, 2, B * F2])
        wfT = sb("wfT", [EMB, 3, D])
        w0 = sb("w0", [EMB, R0])
        w1T = sb("w1T", [8 * F1, 2, EMB])
        w2T = sb("w2T", [F2, GP, EMB])
        bcol = sb("bcol", [EMB, 3])
        bfrow = sb("bfrow", [1, D])
        ones = sb("ones", [1, 128])
        y1T, y2T = sb("y1T", [EMB, B * G1]), sb("y2T", [EMB, B * G2])
        z1, z2 = sb("z1", [128, B // 2, D]), sb("z2", [128, D])
        fused = sb("fused", [128, B, D])
        patches = sb("patches", [128, 2, 128])
        patchesT = sb("patchesT", [128, NTOK])

        h = sb("h", [128, T, D])
        stats, meanvar, rstd = sb("stats", [128, T, 6]), sb("meanvar", [128, T, 2]), sb("rstd", [128, 2, T])
        negmean = sb("negmean", [128, T])
        minushalf = sb("minushalf", [128, T])
        xn = sb("xn", [128, T, D])
        resid = sb("resid", [128, 2, T, D])
        xT0, xT1 = sb("xT0", [DC, S]), sb("xT1", [DC, S])
        wqk0, wqk1 = sb("wqk0", [DC, 3, 128]), sb("wqk1", [DC, 3, 128])
        wv0, wv1 = sb("wv0", [DC, D]), sb("wv1", [DC, D])
        bqk = sb("bqk", [128, 3])
        qkscale = sb("qkscale", [128, 3])
        bvrow, borow, b2row = sb("bvrow", [128, D]), sb("borow", [128, D]), sb("b2row", [128, D])
        full = sb("full", [128, 2, S])
        rest = sb("rest", [128, 2, S])
        parts = sb("parts", [128, 3, 3, S], BF16)
        stackq = sb("stackq", [SLOTS * DH, 2, H, S], BF16)
        stackk = sb("stackk", [SLOTS * DH, 2, H, S], BF16)
        rows1b = full[:].rearrange("p k n -> p (k n)").rearrange("p (b x) -> p b x", b=B)
        t1T = stackk[:, 1].rearrange("p h n -> p (h n)").bitcast(F32)[:, 0:B * 128].rearrange(
            "p (b t) -> p b t", b=B)
        t2T = stackq[0:F2, 1].rearrange("p h n -> p (h n)").bitcast(F32)[:, 0:2 * B * 128].rearrange(
            "p (j b t) -> p j b t", j=2, b=B)
        v = sb("v", [128, 2, T, D])
        negmax, sums, inv = sb("negmax", [128, 3, 2]), sb("sums", [128, 9, 4]), sb("inv", [128, 9, 4])
        probs = sb("probs", [128, 9, 2, S])
        vs = sb("vs", [128, 3, 4, 32])
        ctxT = sb("ctxT", [128, GROUPS, S])
        wo = sb("wo", [128, GROUPS, D])
        h2 = sb("h2", [128, T, D])
        stats2, meanvar2, rstd2 = sb("stats2", [128, T, 6]), sb("meanvar2", [128, T, 2]), sb("rstd2", [128, 2, T])
        negmean2 = sb("negmean2", [128, T])
        xn2 = sb("xn2", [128, T, D])
        xr = sb("xr", [128, T, D])
        xhi, xq = sb("xhi", [128, T, D], BF16), sb("xq", [128, T, D], BF16)
        resid2 = sb("resid2", [128, B * T, D])
        xqT0, xqT1 = sb("xqT0", [DC, B * S], BF16), sb("xqT1", [DC, B * S], BF16)

        early = resid2[:].rearrange("p n d -> p (n d)")
        w1f0, w1f1 = early[0:DC, 0:HID], early[0:DC, HID:2 * HID]
        aw1row, aa2row = early[:, 2 * HID:3 * HID], early[:, 3 * HID:4 * HID]
        w2f = early[:, 4 * HID:4 * HID + MH * D].rearrange("p (m d) -> p m d", m=MH)
        w1q0, w1q1 = sb("w1q0", [DC, HID], BF16), sb("w1q1", [DC, HID], BF16)
        w2q = sb("w2q", [128, MH, D], BF16)
        aw2row, aa1row = sb("aw2row", [128, D]), sb("aa1row", [128, D])
        aw1col, b1col = sb("aw1col", [128, MH]), sb("b1col", [128, MH])
        mean1, mean2 = sb("mean1", [128, 1]), sb("mean2", [128, 1])
        inv1, inv2 = sb("inv1", [128, 1]), sb("inv2", [128, 1])
        top2, low2 = sb("top2", [128, 1]), sb("low2", [128, 1])
        scale1 = sb("scale1", [128, MH])
        scale2 = sb("scale2", [128, D])
        spare = probs[:].rearrange("p r j n -> p (r j) n")
        act_, rounded = spare[:, 0:3], spare[:, 3:6]
        hhi = sb("hhi", [128, 3, S], BF16)
        hq = sb("hq", [128, 2, MH, S], BF16)
        scaled, result = (spare[:, k:k + 3].rearrange("p r n -> p (r n)").rearrange("p (q t d) -> p q t d", q=2, t=T)
                          for k in (6, 9))

        cut = nc.dram_tensor("cut", (2, 2, 3, DH, H, S), BF16, kind="Internal").ap()

        PS = ctx.enter_context(nc.psum_tensor("PS", [128, 8, 512], F32))
        CTX, MISC = 6, 7

        def bank_of(step, body):
            ahead = {"qk0": 0, "qk1": 1, "qk2": 2, "v01": 3, "v2": 4}
            return ahead.get(step, MISC) if isinstance(body, int) and body == -2 else MISC

        miscb = PS[:, MISC, :].bitcast(BF16)

        idx_in, consts_in = sem("idx_in"), sem("consts_in")
        tokw_in, attw_in, ffnw_in = sem("tokw_in"), sem("attw_in"), sem("ffnw_in")
        got2, got1, got0 = sem("got2"), sem("got1"), sem("got0")
        pe_set, dve_set = sem("pe_set"), sem("dve_set")
        prep_chain = sem("prep_chain")
        pool_set, pool_chain = sem("pool_set"), sem("pool_chain")
        fused_in, text_in = sem("fused_in"), sem("text_in")
        patches_in = sem("patches_in")
        bank_full = sem("bank_full")
        vector_read, scalar_read = sem("vector_read"), sem("scalar_read")
        stats_in, meanvar_in, text_used = sem("stats_in"), sem("meanvar_in"), sem("text_used")
        var_in, rstd_in, negmean_in, xn_in = sem("var_in"), sem("rstd_in"), sem("negmean_in"), sem("xn_in")
        part1_in, rest_in, part2_in, part3_in = sem("part1_in"), sem("rest_in"), sem("part2_in"), sem("part3_in")
        cut_in = [sem(f"cut_in{mt}") for mt in range(3)]
        stack_in = [[sem(f"stack_in{p}{half}") for half in range(2)] for p in range(2)]
        scores_in, max_in, exp_in, inv_in, vs_in = (sem("scores_in"), sem("max_in"), sem("exp_in"),
                                                   sem("inv_in"), sem("vs_in"))
        pv_done, ctx_in = sem("pv_done"), sem("ctx_in")
        stats2_in, meanvar2_in = sem("stats2_in"), sem("meanvar2_in")
        var2_in, rstd2_in, negmean2_in, xn2_in = sem("var2_in"), sem("rstd2_in"), sem("negmean2_in"), sem("xn2_in")
        xr_in, xhi_in, xq_in, resid2_in = sem("xr_in"), sem("xhi_in"), sem("xq_in"), sem("resid2_in")
        hid_in, gelu_in, rounded_in, hhi_in, hq_in = (sem("hid_in"), sem("gelu_in"), sem("rounded_in"),
                                                      sem("hhi_in"), sem("hq_in"))
        ffn_in, scaled_in, result_in, stored = sem("ffn_in"), sem("scaled_in"), sem("result_in"), [sem("stored0"), sem("stored1")]

        N_TOKW, N_ATTW, N_FFNW = 8, 9, 9

        block = ctx.enter_context(nc.Block())

        @block.sync
        def _(sp):
            for dst, src in ((x2i, "idx2"), (x1i, "idx1"), (x0i, "idx0")):
                sp.dma_start(dst[:], a[src]).then_inc(idx_in, 16)
            sp.dma_start(ident[:], a["ident"]).then_inc(consts_in, 16)
            sp.dma_start(patches[:, :, R0:128], a["interp"]).then_inc(consts_in, 16)
            for dst, src in ((w2T, "W2T"), (w1T, "W1T"), (w0, "W0"), (wfT, "WfT")):
                sp.dma_start(dst[:], a[src]).then_inc(tokw_in, 16)
            for n in range(3):
                sp.dma_start(bcol[:, n:n + 1], a[f"b{n}"]).then_inc(tokw_in, 16)
            sp.dma_start(bfrow[:], a["bf"]).then_inc(tokw_in, 16)
            sp.dma_start(h[:, 2, :], a["txt"][0]).then_inc(text_in, 16)
            sp.wait_ge(dve_set, Z2_COPIED)
            for b in range(B):
                sp.dma_start(fused[128 - G2:128, b, :], z2[G2 * b:G2 * (b + 1), :]).then_inc(fused_in, 16)
            sp.wait_ge(dve_set, Z1_COPIED)
            f = fused[R0:R0 + G1, :, :].rearrange("p (q r) d -> p r q d", r=2)
            for r in range(2):
                sp.dma_start(f[:, r], z1[G1 * r:G1 * (r + 1), :, :]).then_inc(fused_in, 16)

            def store_parts(c, p, mt):
                wait_behind(sp, (idx_in, 48), (part1_in, 3 * c + mt + 1),
                            (stack_in[p][0 if mt < 2 else 1], earlier(16 * 2 * len(RUNS), c, p)))
                for part, ready in enumerate((part1_in, part2_in, part3_in)):
                    if part > 0:
                        sp.wait_ge(ready, 3 * c + mt + 1)
                    for k, first, n, h0 in (((mt, 0, 8, 0),) if mt < 2 else ((0, 0, 4, 8), (1, 64, 4, 8))):
                        sp.dma_start(cut[p, k, part, :, h0:h0 + n, :].rearrange("e h n -> h e n"),
                                     parts[first:first + DH * n, mt, part, :]).then_inc(cut_in[mt], 16)

            def load_stacks(c, p, half):
                if half == 0:
                    wait_behind(sp, (idx_in, 48), (scores_in, PAIRS * (c - 1)), (cut_in[0], 16 * 3 * (c + 1)),
                                (cut_in[1], 16 * 3 * (c + 1)))
                else:
                    wait_behind(sp, (idx_in, 48), (scores_in, PAIRS * (c - 1)), (cut_in[2], 16 * 6 * (c + 1)))
                h0, n = ((0, 8), (8, 4))[half]
                for s, k in RUNS:
                    rows = slice(DH * s, DH * (s + k))
                    part = PARTS_Q[s]
                    sp.dma_start(stackq[rows, p, h0:h0 + n, :],
                                 cut[p, 0, part:part + 1, :, h0:h0 + n, :].broadcast_to([k, DH, n, S])).then_inc(stack_in[p][half], 16)
                    sp.dma_start(stackk[rows, p, h0:h0 + n, :], cut[p, 1, 0:k, :, h0:h0 + n, :]).then_inc(stack_in[p][half], 16)

            def stacks(c, p, more=True):
                for mt in range(3):
                    store_parts(c, p, mt)
                    if mt == 1 and more:
                        text(c + 1)
                    if mt > 0:
                        load_stacks(c, p, mt - 1)

            def text(c):
                wait(sp, text_used, c)
                wait(sp, meanvar_in, c)
                sp.dma_start(h[:, 2, :], a["txt"][c]).then_inc(text_in, 16)

            stacks(0, 0)
            stacks(1, 1)
            with sp.Fori(1, B // 2 - 1) as i:
                for p in range(2):
                    stacks(2 * i + p, p)
            stacks(B - 2, 0)
            stacks(B - 1, 1, more=False)

            def store(b, p):
                sp.wait_ge(result_in, b + 1)
                sp.dma_start(out[b], result[:, p]).then_inc(stored[p], 16)

            with sp.Fori(0, B // 2) as i:
                for p in range(2):
                    store(2 * i + p, p)
            for p in range(2):
                sp.wait_ge(stored[p], 16 * (B // 2))

        @block.gpsimd
        def _(pool):
            nc.gpsimd.memset(ones[:], 1.0).then_inc(pool_set, 1)
            nc.gpsimd.memset(minushalf[:], -0.5).then_inc(pool_set, 1)
            nc.gpsimd.memset(vs[:], 0.0).then_inc(pool_set, 1)
            pool.wait_ge(idx_in, 48)

            def gather(dst, table, idx, done):
                nc.gpsimd.indirect_dma_start(dst, None, table, bass.IndirectOffsetOnAxis(ap=idx, axis=0)).then_inc(done, 16)

            for jh in range(2):
                gather(rows2[:, jh, :], a["table2"], x2i[:, jh:jh + 1], got2)
            for j in range(8):
                gather(rows1[:, j, :], a["table1"], x1i[:, j:j + 1], got1)
            for t in range(2):
                for j in range(GP):
                    gather(rows0[:, t, j, :], a["table0"], x0i[:, t, j:j + 1], got0)

            def patch_columns(c):
                wait(pool, meanvar_in, c)
                nc.gpsimd.tensor_copy(
                    patches[:, :, 0:R0].rearrange("p t (j c) -> p t j c", c=F0),
                    rows0[:, :, :, bass.ds(F0 * c, F0)]).then_inc(patches_in, 1)

            def layernorm(c, p):
                wait_behind(pool, (pool_set, 3), (meanvar_in, c + 1))
                nc.gpsimd.tensor_scalar(rstd[:, 0, :], meanvar[:, :, 1], 1.0, EPS, ALU.mult, ALU.add).then_inc(var_in, 1)
                nc.gpsimd.tensor_scalar(negmean[:], meanvar[:, :, 0], -1.0, 0.0, ALU.mult, ALU.add).then_inc(negmean_in, 1)
                pool.wait_ge(var_in, c + 1)
                nc.gpsimd.tensor_tensor(out=rstd[:, 1, :], in0=rstd[:, 0, :], in1=minushalf[:], op=ALU.pow).then_inc(rstd_in, 1)
                wait_behind(pool, (pool_set, 3), (rstd_in, c + 1), (negmean_in, c + 1), (part1_in, 3 * c))
                for t in range(T):
                    nc.gpsimd.tensor_scalar(xn[:, t, :], h[:, t, :], negmean[:, t:t + 1], rstd[:, 1, t:t + 1],
                                            ALU.add, ALU.mult).then_inc(xn_in, 1)

            def residual(c, p):
                wait(pool, stats2_in, T * (c - 1))
                nc.gpsimd.tensor_tensor(out=resid[:, p], in0=h[:], in1=borow[:].unsqueeze(1).broadcast_to([128, T, D]),
                                        op=ALU.add).then_inc(text_used, 1)

            def rest_after_part1(c, mt):
                pool.wait_ge(part1_in, 3 * c + mt + 1)
                k = mt % 2
                wait(pool, part3_in, 3 * c + (0, -1, 1)[mt])
                nc.gpsimd.tensor_tensor(out=rest[:, k], in0=full[:, k], in1=parts[:, mt, 0], op=ALU.subtract).then_inc(rest_in, 1)

            def part3(c, mt):
                pool.wait_ge(part2_in, 3 * c + mt + 1)
                k = mt % 2
                nc.gpsimd.tensor_tensor(out=parts[:, mt, 2], in0=rest[:, k], in1=parts[:, mt, 1], op=ALU.subtract).then_inc(part3_in, 1)

            def scale_values(b, p, n):
                g, t, r = n // 3, n % 3, n % 3
                pool.wait_ge(inv_in, BLOCKS * b + n + 1)
                wait(pool, pv_done, BLOCKS * b + n - 2)
                nc.gpsimd.tensor_tensor(
                    out=vs[:, r, :, 0:DH], in0=v[:, p, t, 4 * DH * g:4 * DH * (g + 1)].rearrange("p (h e) -> p h e", e=DH),
                    in1=inv[:, n, :].unsqueeze(2).broadcast_to([128, 4, DH]), op=ALU.mult).then_inc(vs_in, 1)

            def layernorm2(b):
                wait_behind(pool, (pool_set, 3), (meanvar2_in, b + 1))
                nc.gpsimd.tensor_scalar(rstd2[:, 0, :], meanvar2[:, :, 1], 1.0, EPS, ALU.mult, ALU.add).then_inc(var2_in, 1)
                nc.gpsimd.tensor_scalar(negmean2[:], meanvar2[:, :, 0], -1.0, 0.0, ALU.mult, ALU.add).then_inc(negmean2_in, 1)
                pool.wait_ge(var2_in, b + 1)
                nc.gpsimd.tensor_tensor(out=rstd2[:, 1, :], in0=rstd2[:, 0, :], in1=minushalf[:], op=ALU.pow).then_inc(rstd2_in, 1)
                wait_behind(pool, (pool_set, 3), (rstd2_in, b + 1), (negmean2_in, b + 1))
                for t in range(T):
                    nc.gpsimd.tensor_scalar(xn2[:, t, :], h2[:, t, :], negmean2[:, t:t + 1], rstd2[:, 1, t:t + 1],
                                            ALU.add, ALU.mult).then_inc(xn2_in, 1)
                wait_behind(pool, (pool_set, 3), (xn2_in, 3 * b + 3))
                nc.gpsimd.tensor_scalar(xr[:], xn2[:], inv1[:], ROUND, ALU.mult, ALU.add).then_inc(xr_in, 1)

            def residual2(b):
                nc.gpsimd.tensor_tensor(out=resid2[:, bass.ds(T * b, T), :], in0=h2[:],
                                        in1=b2row[:].unsqueeze(1).broadcast_to([128, T, D]), op=ALU.add).then_inc(resid2_in, 1)

            pool.wait_ge(got0, 16 * 2 * GP)
            pool.wait_ge(consts_in, 32)
            patch_columns(0)
            pool.wait_ge(attw_in, 16 * N_ATTW)
            layernorm(0, 0)
            residual(0, 0)
            patch_columns(1)
            rest_after_part1(0, 0)
            rest_after_part1(0, 1)
            part3(0, 0)
            rest_after_part1(0, 2)
            part3(0, 1)
            part3(0, 2)

            def body(b, p, front=True, back=True, tail=True):
                c, o, q = b + 1, b - 1, 1 - p
                for k in range(PAIRS):
                    due = [name for name in ON_GPSIMD if ON_GPSIMD[name] == k]
                    if k % 2 == VALUES_LAG % 2:
                        if k >= VALUES_LAG:
                            scale_values(b, p, (k - VALUES_LAG) // 2)
                        elif tail:
                            scale_values(o, q, BLOCKS + (k - VALUES_LAG) // 2)
                    if "patches" in due and front:
                        patch_columns(b + 2)
                    if "layernorm" in due and back:
                        layernorm(c, q)
                    if "residual" in due and back:
                        residual(c, q)
                    if "layernorm2" in due and tail:
                        layernorm2(o)
                    if "rest0" in due and back:
                        rest_after_part1(c, 0)
                    if "rest1" in due and back:
                        rest_after_part1(c, 1)
                    if "part30" in due and back:
                        part3(c, 0)
                    if "rest2" in due and back:
                        rest_after_part1(c, 2)
                    if "part31" in due and back:
                        part3(c, 1)
                    if "part32" in due and back:
                        part3(c, 2)
                    if "residual2" in due and tail:
                        residual2(o)

            pool.wait_ge(dve_set, WEIGHTS_READY)
            body(0, 0, tail=False)
            with pool.Fori(0, (B - 4) // 2) as i:
                body(2 * i + 1, 1)
                body(2 * i + 2, 0)
            body(B - 3, 1)
            body(B - 2, 0, front=False)
            body(B - 1, 1, front=False, back=False)
            for n in range((PAIRS - VALUES_LAG + 1) // 2, BLOCKS):
                scale_values(B - 1, 1, n)

            def round_hidden(b, m):
                r = m % 3
                wait_behind(pool, (pool_set, 3), (gelu_in, MH * b + m + 1), (hhi_in, MH * b + m - 2))
                nc.gpsimd.tensor_scalar(rounded[:, r], act_[:, r], inv2[:], ROUND, ALU.mult, ALU.add).then_inc(rounded_in, 1)

            for m in range(MH):
                if m == 3:
                    layernorm2(B - 1)
                round_hidden(0, m)
            residual2(B - 1)
            with pool.Fori(1, B) as i:
                for m in range(MH):
                    round_hidden(i, m)

        @block.scalar
        def _(act):
            for dst, src in ((aw1row, "aw1row"), (aw2row, "aw2row"), (aa1row, "aa1row"), (aa2row, "aa2row"),
                             (aw1col, "aw1col"), (b1col, "b1col"), (w1f0, "w1f0"), (w1f1, "w1f1"), (w2f, "w2f")):
                act.dma_start(dst[:], a[src]).then_inc(ffnw_in, 16)
            for dst, src in ((wqk0, "wqk0"), (wqk1, "wqk1"), (wv0, "wv0"), (wv1, "wv1"), (bqk, "bqk"), (wo, "wo"),
                             (bvrow, "bvrow"), (borow, "borow"), (b2row, "b2row")):
                act.dma_start(dst[:], a[src]).then_inc(attw_in, 16)

            def full_bank(step, body):
                act.wait_ge(bank_full, steps_before(step, body) + 1)

            def read_tokens(c, body):
                full_bank("tokens", body)
                wait(act, text_used, c)
                nc.scalar.copy(h[:, 0:2, :], PS[:, MISC, 0:2 * D].rearrange("p (t d) -> p t d", t=2)).then_inc(scalar_read, 1)

            def read_x(part, body):
                full_bank(f"turn_x{part}", body)
                nc.scalar.copy((xT0, xT1)[part][:], PS[0:DC, MISC, 0:S]).then_inc(scalar_read, 1)

            def read_context(b, g, tail):
                act.wait_ge(pv_done, BLOCKS * b + 3 * g + 3)
                if g == 0 and tail:
                    act.wait_ge(bank_full, steps_before("out2", b) + 1)
                nc.scalar.copy(ctxT[:, g, :], PS[:, CTX, 0:S]).then_inc(ctx_in, 1)

            def body(b, front=True, back=True, tail=True):
                for k in range(PAIRS):
                    q = k % 3
                    if k % 2 == 1:
                        wait(act, pv_done, BLOCKS * b + (k - 9) // 2 + 1)
                    act.wait_ge(max_in, PAIRS * b + k + 1)
                    for j in range(2):
                        done = nc.scalar.activation(probs[:, k % 9, j, :], PS[:, 2 * q + j, 0:S], ACT.Exp,
                                                    bias=negmax[:, q, j:j + 1],
                                                    accum_out=sums[:, k // 2, 2 * (k % 2) + j:2 * (k % 2) + j + 1])
                    done.then_inc(exp_in, 1)
                    if k == ON_SCALAR["tokens"] and front:
                        read_tokens(b + 2, b)
                    group, late = divmod(k - ON_SCALAR["context"], 6)
                    if late == 0 and group >= 0:
                        read_context(b, group, tail)
                    elif late == 0 and tail:
                        read_context(b - 1, GROUPS + group, True)
                    for part in range(2):
                        if k == ON_SCALAR[f"turn_x{part}"] and back:
                            read_x(part, b)

            read_tokens(0, -2)
            read_x(0, -2)
            read_x(1, -2)
            read_tokens(1, -1)
            body(0, tail=False)
            with act.Fori(1, B - 2) as i:
                body(i)
            body(B - 2, front=False)
            body(B - 1, front=False, back=False)
            read_context(B - 1, 2, True)

            def gelu(b, m):
                wait(act, rounded_in, MH * b + m - 2)
                act.wait_ge(hid_in, MH * b + m + 1)
                nc.scalar.activation(act_[:, m % 3], PS[:, m % 3, 0:S], ACT.Gelu, bias=b1col[:, m:m + 1],
                                     scale=scale1[:, m:m + 1]).then_inc(gelu_in, 1)

            for m in range(MH):
                gelu(0, m)
            with act.Fori(1, B) as i:
                for m in range(MH):
                    gelu(i, m)

        @block.vector
        def _(dve):
            chain = [0]

            def link(instruction):
                chain[0] += 1
                instruction.then_inc(prep_chain, 1)
                dve.wait_ge(prep_chain, chain[0])

            dve.wait_ge(consts_in, 32)
            nc.vector.tensor_copy(identb[:], ident[:]).then_inc(dve_set, 1)
            nc.vector.memset(qkscale[:], 1.0).then_inc(prep_chain, 1)
            chain[0] += 1
            dve.wait_ge(prep_chain, 1)
            link(nc.vector.memset(qkscale[:, 0:1], DH ** -0.5))
            link(nc.vector.memset(qkscale[0:64, 2:3], DH ** -0.5))

            for n in range(4):
                dve.wait_ge(pe_set, n + 1)
                nc.vector.tensor_copy(t2T[:, n // 2, 4 * (n % 2):4 * (n % 2) + 4, :],
                                      PS[0:F2, n, :].rearrange("p (b t) -> p b t", b=4)).then_inc(dve_set, 1)
            dve.wait_ge(ffnw_in, 16 * N_FFNW)
            link(nc.vector.tensor_reduce(out=mean1[:], in_=aa1row[:], axis=AX.X, op=ALU.add))
            link(nc.vector.tensor_scalar(mean1[:], mean1[:], 1.0 / D, None, ALU.mult))
            link(nc.vector.tensor_reduce(out=mean2[:], in_=aa2row, axis=AX.X, op=ALU.add))
            link(nc.vector.tensor_scalar(mean2[:], mean2[:], 1.0 / HID, None, ALU.mult))
            link(nc.vector.reciprocal(inv1[:], mean1[:]))
            link(nc.vector.reciprocal(inv2[:], mean2[:]))
            link(nc.vector.tensor_scalar(scale1[:], aw1col[:], mean1[:], None, ALU.mult))
            link(nc.vector.tensor_scalar(scale2[:], aw2row[:], mean2[:], None, ALU.mult))
            link(nc.vector.tensor_scalar(top2[:], inv2[:], CLIP, QP, ALU.mult, ALU.min))
            link(nc.vector.tensor_scalar(top2[:], top2[:], ROUND, ROUND, ALU.add, ALU.subtract))
            link(nc.vector.tensor_scalar(low2[:], inv2[:], -CLIP, QN, ALU.mult, ALU.max))
            link(nc.vector.tensor_scalar(low2[:], low2[:], ROUND, ROUND, ALU.add, ALU.subtract))
            link(nc.vector.reciprocal(aw1row, aw1row))
            link(nc.vector.reciprocal(aw2row[:], aw2row[:]))
            dve.wait_ge(pe_set, 5)
            dve.wait_ge(tokw_in, 16 * N_TOKW)
            nc.vector.tensor_scalar(y2T[:], PS[0:EMB, 4, 0:B * G2], bcol[:, 2:3], None, ALU.add).then_inc(dve_set, 1)
            dve.wait_ge(pe_set, 6)
            nc.vector.tensor_copy(z2[:], PS[:, 5, 0:D]).then_inc(dve_set, 1)
            dve.wait_ge(pe_set, 7)
            nc.vector.tensor_copy(fused[0:R0, :, :], PS[0:R0, 6, 0:D].unsqueeze(1).broadcast_to([R0, B, D])).then_inc(dve_set, 1)
            dve.wait_ge(got1, 16 * 8)
            nc.vector.tensor_copy(rows1b.rearrange("p b (j f) -> p j b f", j=8),
                                  rows1[:].rearrange("p j (b f) -> p j b f", b=B)).then_inc(dve_set, 1)
            for n in range(2):
                dve.wait_ge(pe_set, 8 + n)
                nc.vector.tensor_copy(t1T[:, 4 * n:4 * n + 4, :],
                                      PS[0:8 * F1, n, :].rearrange("p (b t) -> p b t", b=4)).then_inc(dve_set, 1)
            dve.wait_ge(pe_set, 10)
            nc.vector.tensor_scalar(y1T[:], PS[0:EMB, 2, :], bcol[:, 1:2], None, ALU.add).then_inc(dve_set, 1)
            for n in range(2):
                dve.wait_ge(pe_set, 11 + n)
                nc.vector.tensor_copy(z1[:, 2 * n:2 * n + 2, :],
                                      PS[:, 3 + n, 0:2 * D].rearrange("p (q d) -> p q d", q=2)).then_inc(dve_set, 1)

            for w, wq, r in ((w1f0, w1q0[:], aw1row[0:DC]), (w1f1, w1q1[:], aw1row[0:DC]),
                             (w2f, w2q[:], aw2row[:].unsqueeze(1).broadcast_to([128, MH, D]))):
                link(nc.vector.tensor_tensor(out=w, in0=w, in1=r, op=ALU.mult))
                link(nc.vector.tensor_scalar(w, w, QN, QP, ALU.max, ALU.min))
                link(nc.vector.tensor_scalar(wq, w, ROUND, ROUND, ALU.add, ALU.subtract))
            nc.vector.memset(h2[:, 0, 0:1], 0.0).then_inc(dve_set, 1)

            def full_bank(step, body):
                dve.wait_ge(bank_full, steps_before(step, body) + 1)

            def own_read(step, body):
                dve.wait_ge(vector_read, steps_before(step, body, same_reader(step)) + 1)

            def read_patches(c, p, body):
                full_bank("turn_patches", body)
                nc.vector.tensor_copy(patchesT[:], PS[:, MISC, 0:NTOK]).then_inc(vector_read, 1)

            def token_stats(c, body):
                dve.wait_ge(scalar_read, steps_before("tokens", body, BY_SCALAR) + 1)
                dve.wait_ge(text_in, 16 * c + 16)
                for t in range(T):
                    nc.vector.bn_stats(stats[:, t, :], h[:, t, :]).then_inc(stats_in, 1)

            def token_stats_ready(c):
                dve.wait_ge(stats_in, T * c + T)

            def token_meanvar(c):
                for t in range(T):
                    done = nc.vector.bn_aggr(meanvar[:, t, :], stats[:, t, :])
                done.then_inc(meanvar_in, 1)

            def read_qk(c, mt, body):
                full_bank(f"qk{mt}", body)
                k = mt % 2
                wait(dve, rest_in, 3 * c + (0, -1, 1)[mt])
                nc.vector.tensor_scalar(full[:, k], PS[:, bank_of(f"qk{mt}", body), 0:S], bqk[:, mt:mt + 1], qkscale[:, mt:mt + 1],
                                        ALU.add, ALU.mult).then_inc(vector_read, 1)

            def part1(c, mt, body):
                own_read(f"qk{mt}", body)
                wait(dve, cut_in[mt], 16 * 3 * (2 if mt == 2 else 1) * c)
                nc.vector.tensor_copy(parts[:, mt, 0], full[:, mt % 2]).then_inc(part1_in, 1)

            def part2(c, mt):
                dve.wait_ge(rest_in, 3 * c + mt + 1)
                nc.vector.tensor_copy(parts[:, mt, 1], rest[:, mt % 2]).then_inc(part2_in, 1)

            def read_v(c, p, step, body):
                full_bank(step, body)
                wait(dve, vs_in, BLOCKS * (c - 1))
                t, n = (0, 2) if step == "v01" else (2, 1)
                nc.vector.tensor_tensor(out=v[:, p, t:t + n, :], in0=PS[:, bank_of(step, body), 0:n * D].rearrange("p (t d) -> p t d", t=n),
                                        in1=bvrow[:].unsqueeze(1).broadcast_to([128, n, D]), op=ALU.add).then_inc(vector_read, 1)

            def negative_max(b, n):
                q = n % 3
                dve.wait_ge(scores_in, PAIRS * b + n + 1)
                nc.vector.tensor_reduce(out=negmax[:, q, :], in_=PS[:, 2 * q:2 * q + 2, 0:S], axis=AX.X, op=ALU.max,
                                        negate=True).then_inc(max_in, 1)

            def inverse_sums(b, n):
                dve.wait_ge(exp_in, PAIRS * b + 2 * n + 2)
                nc.vector.reciprocal(inv[:, n, :], sums[:, n, :]).then_inc(inv_in, 1)

            def read_out(b, p, step, body):
                full_bank(step, body)
                wait(dve, resid2_in, b)
                t, n = (0, 2) if step == "out01" else (2, 1)
                nc.vector.tensor_tensor(out=h2[:, t:t + n, :], in0=PS[:, MISC, 0:n * D].rearrange("p (t d) -> p t d", t=n),
                                        in1=resid[:, p, t:t + n, :], op=ALU.add).then_inc(vector_read, 1)

            def out_stats(b, body):
                own_read("out2", body)
                for t in range(T):
                    nc.vector.bn_stats(stats2[:, t, :], h2[:, t, :]).then_inc(stats2_in, 1)

            def out_stats_ready(b):
                dve.wait_ge(stats2_in, T * b + T)

            def out_meanvar(b):
                for t in range(T):
                    done = nc.vector.bn_aggr(meanvar2[:, t, :], stats2[:, t, :])
                done.then_inc(meanvar2_in, 1)

            def quantise(b):
                dve.wait_ge(xr_in, b + 1)
                nc.vector.tensor_scalar(xhi[:], xr[:], ROUND, QP, ALU.subtract, ALU.min).then_inc(xhi_in, 1)
                dve.wait_ge(xhi_in, b + 1)
                nc.vector.tensor_scalar(xq[:], xhi[:], QN, None, ALU.max).then_inc(xq_in, 1)

            def read_xq(b, body):
                full_bank("turn_xq", body)
                nc.vector.tensor_copy(xqT0[:, bass.ds(S * b, S)], miscb[0:DC, 0:S])
                nc.vector.tensor_copy(xqT1[:, bass.ds(S * b, S)], miscb[0:DC, 512:512 + S]).then_inc(vector_read, 1)

            read_patches(0, 0, -2)
            token_stats(0, -2)
            token_stats_ready(0)
            token_meanvar(0)
            for mt in range(3):
                read_qk(0, mt, -2)
                part1(0, mt, -2)
                if mt > 0:
                    part2(0, mt - 1)
            part2(0, 2)
            read_v(0, 0, "v01", -2)
            read_v(0, 0, "v2", -2)
            read_patches(1, 1, -1)
            token_stats(1, -1)
            token_stats_ready(1)
            token_meanvar(1)

            def body(b, p, front=True, back=True, tail=True):
                c, o, q = b + 1, b - 1, 1 - p
                for k in range(PAIRS):
                    due = [name for name in ON_VECTOR if ON_VECTOR[name] == k]
                    if "token_meanvar" in due and front:
                        token_stats_ready(b + 2)
                    if "out_meanvar" in due and tail:
                        out_stats_ready(o)
                    negative_max(b, k)
                    if "token_meanvar" in due and front:
                        token_meanvar(b + 2)
                    if "out_meanvar" in due and tail:
                        out_meanvar(o)
                    if k % 2 == INV_LAG % 2:
                        if k >= INV_LAG:
                            inverse_sums(b, (k - INV_LAG) // 2)
                        elif tail:
                            inverse_sums(o, BLOCKS + (k - INV_LAG) // 2)
                    if back:
                        for mt in range(3):
                            if f"part2{mt}" in due:
                                part2(c, mt)
                            if f"qk{mt}" in due:
                                read_qk(c, mt, b)
                                part1(c, mt, b)
                        for step in ("v01", "v2"):
                            if step in due:
                                read_v(c, q, step, b)
                    if tail:
                        for step in ("out01", "out2"):
                            if step in due:
                                read_out(o, q, step, b)
                        if "out2" in due:
                            out_stats(o, b)
                        if "quantise" in due:
                            quantise(o)
                        if "turn_xq" in due:
                            read_xq(o, b)
                    if front:
                        if "turn_patches" in due:
                            read_patches(b + 2, p, b)
                        if "token_stats" in due:
                            token_stats(b + 2, b)

            body(0, 0, tail=False)
            with dve.Fori(0, (B - 4) // 2) as i:
                body(2 * i + 1, 1)
                body(2 * i + 2, 0)
            body(B - 3, 1)
            body(B - 2, 0, front=False)
            body(B - 1, 1, front=False, back=False)
            for n in range((PAIRS - INV_LAG + 1) // 2, BLOCKS):
                inverse_sums(B - 1, n)
            def clip_above(b, m):
                r = m % 3
                dve.wait_ge(rounded_in, MH * b + m + 1)
                wait(dve, hq_in, MH * b + m - 2)
                nc.vector.tensor_scalar(hhi[:, r], rounded[:, r], ROUND, top2[:], ALU.subtract, ALU.min).then_inc(hhi_in, 1)

            def clip_below(b, p, m):
                dve.wait_ge(hhi_in, MH * b + m + 1)
                wait(dve, ffn_in, 2 * (b - 1))
                nc.vector.tensor_scalar(hq[:, p, m], hhi[:, m % 3], low2[:], None, ALU.max).then_inc(hq_in, 1)

            def finish(b, p):
                for k, (t, n) in enumerate(((0, 2), (2, 1))):
                    dve.wait_ge(ffn_in, 2 * b + k + 1)
                    nc.vector.tensor_tensor(
                        out=scaled[:, p, t:t + n, :], in0=PS[:, 4 + 2 * p + k, 0:n * D].rearrange("p (t d) -> p t d", t=n),
                        in1=scale2[:].unsqueeze(1).broadcast_to([128, n, D]), op=ALU.mult).then_inc(scaled_in, 1)
                dve.wait_ge(scaled_in, 2 * b + 2)
                dve.wait_ge(resid2_in, b + 1)
                wait(dve, stored[p], earlier(16, b, p))
                nc.vector.tensor_tensor(out=result[:, p], in0=scaled[:, p], in1=resid2[:, bass.ds(T * b, T), :],
                                        op=ALU.add).then_inc(result_in, 1)

            def ffn(b, p, last=True):
                for m in range(MH):
                    clip_above(b, m)
                    if m > 0:
                        clip_below(b, p, m - 1)
                    if last and m == 3:
                        finish(b - 2, p)
                clip_below(b, p, MH - 1)

            read_out(B - 1, 1, "out01", B)
            read_out(B - 1, 1, "out2", B)
            out_stats(B - 1, B)
            out_stats_ready(B - 1)
            out_meanvar(B - 1)
            for m in range(MH):
                clip_above(0, m)
                if m > 0:
                    clip_below(0, 0, m - 1)
                if m == 2:
                    quantise(B - 1)
                    read_xq(B - 1, B)
            clip_below(0, 0, MH - 1)
            ffn(1, 1, last=False)
            ffn(2, 0)
            ffn(3, 1)
            with dve.Fori(2, B // 2) as i:
                ffn(2 * i, 0)
                ffn(2 * i + 1, 1)
            finish(B - 2, 0)
            finish(B - 1, 1)

        @block.tensor
        def _(pe):
            mm = nc.tensor.matmul
            pe.wait_ge(consts_in, 32)
            pe.wait_ge(got2, 32)
            for n in range(4):
                for k in range(4):
                    jh, b = n // 2, 4 * (n % 2) + k
                    done = nc.tensor.transpose(PS[0:F2, n, 128 * k:128 * (k + 1)], rows2[:, jh, F2 * b:F2 * (b + 1)], ident[:])
                done.then_inc(pe_set, 1)
            pe.wait_ge(tokw_in, 16 * N_TOKW)
            pe.wait_ge(dve_set, 5)
            for j in range(GP):
                jh, jl = j // 8, j % 8
                done = mm(PS[0:EMB, 4, 0:B * G2], w2T[:, j, :], t2T[:, jh, :, G2 * jl:G2 * (jl + 1)], start=(j == 0), stop=(j == GP - 1))
            done.then_inc(pe_set, 1)
            pe.wait_ge(dve_set, 6)
            pe.wait_ge(pool_set, 3)
            mm(PS[:, 5, 0:D], y2T[:], wfT[:, 2, :], start=True, stop=False)
            mm(PS[:, 5, 0:D], bcol[:, 0:1].broadcast_to([EMB, 128]), wfT[:, 0, :], start=False, stop=False)
            mm(PS[:, 5, 0:D], ones[:], bfrow[:], start=False, stop=True).then_inc(pe_set, 1)
            mm(PS[0:R0, 6, 0:D], w0[:], wfT[:, 0, :], start=True, stop=True).then_inc(pe_set, 1)
            pe.wait_ge(dve_set, 9)
            for n in range(2):
                for k in range(4):
                    b = 4 * n + k
                    done = nc.tensor.transpose(PS[0:8 * F1, n, 128 * k:128 * (k + 1)], rows1b[:, b, :], ident[:])
                done.then_inc(pe_set, 1)
            pe.wait_ge(dve_set, 11)
            for jh in range(2):
                done = mm(PS[0:EMB, 2, :], w1T[:, jh, :], t1T[:, :, G1 * jh:G1 * (jh + 1)], start=(jh == 0), stop=(jh == 1))
            done.then_inc(pe_set, 1)
            pe.wait_ge(dve_set, 12)
            for n in range(2):
                for k in range(2):
                    q = 2 * n + k
                    done = mm(PS[:, 3 + n, D * k:D * (k + 1)], y1T[:, 128 * q:128 * (q + 1)], wfT[:, 1, :], start=True, stop=True)
                done.then_inc(pe_set, 1)
            pe.wait_ge(attw_in, 16 * N_ATTW)

            def bank_free(step, body):
                order = steps_of(body) if isinstance(body, int) else ALL
                n = order.index(step)
                if bank_of(step, body) != MISC:
                    if step == "qk0":
                        pe.wait_ge(scalar_read, steps_before(step, body, BY_SCALAR))
                    return
                if n == 0 or order[n - 1] in BY_SCALAR:
                    wait(pe, scalar_read, steps_before(step, body, BY_SCALAR))
                if n == 0 or order[n - 1] not in BY_SCALAR:
                    wait(pe, vector_read, steps_before(step, body, same_reader("v2")))

            def turn_patches(c, p, body):
                bank_free("turn_patches", body)
                pe.wait_ge(patches_in, c + 1)
                for t in range(2):
                    done = nc.tensor.transpose(PS[:, MISC, 128 * t:128 * (t + 1)], patches[:, t, :], ident[:])
                done.then_inc(bank_full, 1)

            def tokens(c, p, body):
                bank_free("tokens", body)
                for t in range(2):
                    done = mm(PS[:, MISC, D * t:D * (t + 1)], patchesT[:, 128 * t:128 * (t + 1)],
                              fused[:, bass.ds(c, 1), :].rearrange("p o d -> p (o d)"), start=True, stop=True)
                done.then_inc(bank_full, 1)

            def turn_x(c, p, body, part):
                bank_free(f"turn_x{part}", body)
                pe.wait_ge(xn_in, T * c + T)
                for t in range(T):
                    done = nc.tensor.transpose(PS[0:DC, MISC, 128 * t:128 * (t + 1)], xn[:, t, DC * part:DC * (part + 1)], ident[:])
                done.then_inc(bank_full, 1)

            def qk(c, p, body, mt):
                bank_free(f"qk{mt}", body)
                bank = bank_of(f"qk{mt}", body)
                mm(PS[:, bank, 0:S], wqk0[:, mt, :], xT0[:], start=True, stop=False)
                mm(PS[:, bank, 0:S], wqk1[:, mt, :], xT1[:], start=False, stop=True).then_inc(bank_full, 1)

            def values(c, p, body, tiles, step):
                bank_free(step, body)
                bank = bank_of(step, body)
                for k, t in enumerate(tiles):
                    mm(PS[:, bank, D * k:D * (k + 1)], xT0[:, 128 * t:128 * (t + 1)], wv0[:], start=True, stop=False)
                    done = mm(PS[:, bank, D * k:D * (k + 1)], xT1[:, 128 * t:128 * (t + 1)], wv1[:], start=False, stop=True)
                done.then_inc(bank_full, 1)

            def project_out(b, body, tiles, step):
                bank_free(step, body)
                pe.wait_ge(ctx_in, GROUPS * b + GROUPS)
                for k, t in enumerate(tiles):
                    for g in range(GROUPS):
                        done = mm(PS[:, MISC, D * k:D * (k + 1)], ctxT[:, g, 128 * t:128 * (t + 1)], wo[:, g, :],
                                  start=(g == 0), stop=(g == GROUPS - 1))
                done.then_inc(bank_full, 1)

            def turn_xq(b, body):
                bank_free("turn_xq", body)
                pe.wait_ge(xq_in, b + 1)
                for t in range(T):
                    nc.tensor.transpose(miscb[0:DC, 128 * t:128 * (t + 1)], xq[:, t, 0:DC], identb[:])
                for t in range(T):
                    done = nc.tensor.transpose(miscb[0:DC, 512 + 128 * t:512 + 128 * (t + 1)], xq[:, t, DC:D], identb[:])
                done.then_inc(bank_full, 1)

            def run(step, b, p, body):
                if step == "turn_patches":
                    turn_patches(b, p, body)
                elif step == "tokens":
                    tokens(b, p, body)
                elif step in ("turn_x0", "turn_x1"):
                    turn_x(b, p, body, int(step[-1]))
                elif step in ("qk0", "qk1", "qk2"):
                    qk(b, p, body, int(step[-1]))
                elif step in ("v01", "v2"):
                    values(b, p, body, (0, 1) if step == "v01" else (2,), step)
                elif step in ("out01", "out2"):
                    project_out(b, body, (0, 1) if step == "out01" else (2,), step)
                else:
                    turn_xq(b, body)

            def scores(b, p, n):
                g, t, k = n // 6, (n % 6) // 2, n % 2
                q = n % 3
                if n % 6 == 0:
                    if g != 1:
                        pe.wait_ge(stack_in[p][g // 2], earlier(16 * 2 * len(RUNS), b, p) + 16 * 2 * len(RUNS))
                wait(pe, exp_in, PAIRS * b + n - 2)
                for j in range(2):
                    head = 4 * g + 2 * k + j
                    done = mm(PS[:, 2 * q + j, 0:S], stackk[:, p, head, 128 * t:128 * (t + 1)], stackq[:, p, head, :],
                              start=True, stop=True)
                done.then_inc(scores_in, 1)

            def context(b, n):
                g, t, r = n // 3, n % 3, n % 3
                pe.wait_ge(vs_in, BLOCKS * b + n + 1)
                if t == 0:
                    wait(pe, ctx_in, GROUPS * b + g)
                for j in range(4):
                    done = mm(PS[32 * j:32 * (j + 1), CTX, 0:S], vs[:, r, j, :], probs[:, (2 * n + j // 2) % 9, j % 2, :],
                              start=(t == 0), stop=(t == 2))
                done.then_inc(pv_done, 1)

            for step in steps_of(-2):
                if step == "tokens":
                    pe.wait_ge(fused_in, 16 * (B + 2))
                    pe.wait_ge(dve_set, 8)
                run(step, 0, 0, -2)
            for step in steps_of(-1):
                run(step, 1, 1, -1)

            def body(b, p, front=True, back=True, tail=True):
                for k in range(PAIRS):
                    scores(b, p, k)
                    for step in ALL:
                        if ON_TENSOR[step] == k:
                            if step in FRONT and front:
                                run(step, b + 2, p, b)
                            elif step in BACK and back:
                                run(step, b + 1, 1 - p, b)
                            elif step in TAIL and tail:
                                run(step, b - 1, 1 - p, b)
                    if k % 2 == CONTEXT_LAG % 2:
                        if k >= CONTEXT_LAG:
                            context(b, (k - CONTEXT_LAG) // 2)
                        elif tail:
                            context(b - 1, BLOCKS + (k - CONTEXT_LAG) // 2)

            pe.wait_ge(vector_read, steps_before("v2", -2, same_reader("v2")) + 1)
            body(0, 0, tail=False)
            with pe.Fori(0, (B - 4) // 2) as i:
                body(2 * i + 1, 1)
                body(2 * i + 2, 0)
            body(B - 3, 1)
            body(B - 2, 0, front=False)
            body(B - 1, 1, front=False, back=False)
            for n in range((PAIRS - CONTEXT_LAG + 1) // 2, BLOCKS):
                context(B - 1, n)
            def hidden(b, m):
                wait(pe, gelu_in, MH * b + m - 2)
                mm(PS[:, m % 3, 0:S], w1q0[:, 128 * m:128 * (m + 1)], xqT0[:, bass.ds(S * b, S)], start=True, stop=False)
                mm(PS[:, m % 3, 0:S], w1q1[:, 128 * m:128 * (m + 1)], xqT1[:, bass.ds(S * b, S)], start=False, stop=True).then_inc(hid_in, 1)

            def back(b, p, t):
                pe.wait_ge(hq_in, MH * b + MH)
                for m in range(MH):
                    done = mm(PS[:, 4 + 2 * p + t // 2, D * (t % 2):D * (t % 2 + 1)], hq[:, p, m, 128 * t:128 * (t + 1)],
                              w2q[:, m, :], start=(m == 0), stop=(m == MH - 1))
                if t > 0:
                    done.then_inc(ffn_in, 1)

            pe.wait_ge(dve_set, WEIGHTS_READY)
            pe.wait_ge(exp_in, PAIRS * B - 1)
            for m in range(MH):
                if m == 3:
                    run("out01", B - 1, 1, B)
                    run("out2", B - 1, 1, B)
                hidden(0, m)
            run("turn_xq", B - 1, 1, B)

            def ffn(b, p):
                for m in range(MH):
                    hidden(b, m)
                    if m >= MH - T:
                        back(b - 1, 1 - p, m - (MH - T))

            ffn(1, 1)
            pe.wait_ge(vector_read, steps_before("turn_xq", B, same_reader("turn_xq")) + 1)
            with pe.Fori(1, B // 2) as i:
                ffn(2 * i, 0)
                ffn(2 * i + 1, 1)
            for t in range(T):
                back(B - 1, 1, t)


Z2_COPIED, Z1_COPIED, WEIGHTS_READY = 7, 14, 15


def interpolation(n_in, n_out):
    pos = np.clip((np.arange(n_out, dtype=np.float32) + 0.5) * (n_in / n_out) - 0.5, 0.0, n_in - 1)
    i0 = np.floor(pos).astype(np.int32)
    i1 = np.minimum(i0 + 1, n_in - 1)
    w = (pos - i0).astype(np.float32)
    m = np.zeros((n_out, n_in), np.float32)
    m[np.arange(n_out), i0] += 1.0 - w
    m[np.arange(n_out), i1] += w
    return m


def kernel(**inputs):
    import concourse.bacc as bacc
    from concourse.bass_utils import run_bass_kernel_spmd

    i = {k: np.asarray(v) for k, v in inputs.items()}
    tok = {k[len("L0_tok_"):]: v for k, v in i.items() if k.startswith("L0_tok_")}
    att = {k[len("L0_attn_"):]: v for k, v in i.items() if k.startswith("L0_attn_")}
    ffn = {k[len("L0_ffn_"):]: v for k, v in i.items() if k.startswith("L0_ffn_")}
    x = i["x"]

    def table(p):
        n = IMG // p
        t = x.reshape(B, CH, n, p, n, p).transpose(2, 4, 0, 3, 5, 1)
        return t.reshape(n * n, B * p * p * CH)

    def heads_first(w):
        return w.transpose(1, 0, 2).reshape(D, H * DH)

    def rows(r):
        return np.broadcast_to(r.reshape(1, -1), (128, r.size))

    wq, wk, wv = (heads_first(att[k]) for k in ("Wq", "Wk", "Wv"))
    bq, bk = att["bq"].reshape(-1), att["bk"].reshape(-1)
    wqk = np.stack([wq[:, :128], wk[:, :128], np.concatenate([wq[:, 128:], wk[:, 128:]], 1)], 1)
    bqk = np.stack([bq[:128], bk[:128], np.concatenate([bq[128:], bk[128:]])], 1)
    wo = np.zeros((4, 32, GROUPS, D), np.float32)
    wo[:, :DH] = att["Wo"].reshape(GROUPS, 4, DH, D).transpose(1, 2, 0, 3)
    arrays = {
        "idx0": tok["idx0"].reshape(2, 128, GP).transpose(1, 0, 2),
        "idx1": tok["idx1"].reshape(G1, 2, 8).transpose(1, 0, 2).reshape(128, 8),
        "idx2": tok["idx2"].reshape(G2, 2, 8).transpose(2, 0, 1).reshape(128, 2),
        "table0": table(1), "table1": table(2), "table2": table(4),
        "ident": np.eye(128, dtype=np.float32),
        "interp": np.concatenate([interpolation(G1, NTOK), interpolation(G2, NTOK)], 1).reshape(2, 128, G1 + G2).transpose(1, 0, 2),
        "W0": tok["W0"],
        "W1T": tok["W1"].T.reshape(2, 8 * F1, EMB).transpose(1, 0, 2),
        "W2T": tok["W2"].T.reshape(GP, F2, EMB).transpose(1, 0, 2),
        "WfT": tok["Wf"].T.reshape(3, EMB, D).transpose(1, 0, 2),
        "b0": tok["b0"].reshape(EMB, 1), "b1": tok["b1"].reshape(EMB, 1), "b2": tok["b2"].reshape(EMB, 1),
        "bf": tok["bf"].reshape(1, D),
        "txt": i["txt"],
        "wqk0": wqk[:DC], "wqk1": wqk[DC:], "wv0": wv[:DC], "wv1": wv[DC:], "bqk": bqk,
        "wo": wo.reshape(128, GROUPS, D),
        "bvrow": rows(att["bv"]), "borow": rows(att["bo"]), "b2row": rows(ffn["b2"]),
        "aa1row": rows(ffn["alpha_a1"]), "aa2row": rows(ffn["alpha_a2"]),
        "w1f0": ffn["w1"].T[:DC], "w1f1": ffn["w1"].T[DC:],
        "w2f": ffn["w2"].T.reshape(MH, 128, D).transpose(1, 0, 2),
        "aw1row": rows(ffn["alpha_w1"]), "aw2row": rows(ffn["alpha_w2"]),
        "aw1col": ffn["alpha_w1"].reshape(MH, 128).T, "b1col": ffn["b1"].reshape(MH, 128).T,
    }
    arrays = {k: np.ascontiguousarray(v) for k, v in arrays.items()}
    nc = bacc.Bacc("TRN2", target_bir_lowering=False, num_devices=1)
    given = {k: nc.dram_tensor(f"in_{k}", v.shape, mybir.dt.from_np(v.dtype), kind="ExternalInput").ap() for k, v in arrays.items()}
    out = nc.dram_tensor("out", (B, S, D), F32, kind="ExternalOutput").ap()
    build(nc, given, out.rearrange("b (t p) d -> b p t d", p=128))
    r = run_bass_kernel_spmd(nc, [{f"in_{k}": v for k, v in arrays.items()}], core_ids=[0])
    return r.results[0]["out"]
```

```python
from contextlib import ExitStack

import numpy as np

import concourse.bass as bass
from concourse import mybir

F32, BF16, I32 = mybir.dt.float32, mybir.dt.bfloat16, mybir.dt.int32
ALU = mybir.AluOpType
ACT = mybir.ActivationFunctionType
AX = mybir.AxisListType

B, CH, IMG = 8, 3, 64
GP = 16
NTOK, NTXT, D = 256, 128, 192
S = NTOK + NTXT
T = S // 128
EMB = 64
H, DH = 12, 16
HID = 768
MH = HID // 128
MP = MH // 2
DC = D // 2
F0, F1, F2 = CH, 4 * CH, 16 * CH
G1, G2 = 64, 16
P1 = (IMG // 2) ** 2
R0 = GP * F0
GROUPS, BLOCKS, PAIRS = 3, 9, 18
EPS = 1e-5
ROUND = 1.5 * 2.0 ** 23
QN, QP, CLIP = -8.0, 7.0, 10.0
PARTS_K = (0, 1, 2, 0, 1, 0)
PARTS_Q = (0, 0, 0, 1, 1, 2)
SLOTS = len(PARTS_K)
RUNS = ((0, 3), (3, 2), (5, 1))
LOADS = (16 * 6, 16 * 8)

FRONT = ["turn_patches", "tokens"]
BACK = ["turn_x0", "turn_x1", "qk0", "qk1", "qk2", "v01", "v2"]
TAIL = ["out01", "out2", "turn_xq"]
ALL = ["turn_x0", "turn_x1", "qk0", "out01", "out2", "qk1", "qk2", "turn_patches", "v01", "tokens", "v2",
       "turn_xq"]
BY_SCALAR = ("tokens", "turn_x0", "turn_x1")
ON_TENSOR = {"turn_x0": 0, "turn_x1": 1, "qk0": 3, "out01": 5, "out2": 7, "qk1": 7, "qk2": 10,
             "turn_patches": 11, "v01": 13, "tokens": 14, "v2": 15, "turn_xq": 17}
ON_VECTOR = {"qk0": 4, "out01": 5, "out2": 7, "out_meanvar": 11, "qk1": 8, "qk2": 10, "part20": 5,
             "part21": 10, "part22": 12, "turn_patches": 12, "token_stats": 14, "token_meanvar": 15,
             "v01": 13, "v2": 15, "quantise": 16, "turn_xq": 17}
ON_SCALAR = {"turn_x0": 0, "turn_x1": 0, "tokens": 12, "context": 9}
ON_GPSIMD = {"layernorm": 14, "residual": 8, "rest0": 5, "part30": 6, "rest1": 9, "rest2": 10,
             "part31": 10, "part32": 11, "patches": 10, "layernorm2": 13, "residual2": 16}
INV_LAG, VALUES_LAG, CONTEXT_LAG = 3, 4, 6


def steps_of(body):
    if body == -2:
        return FRONT + BACK
    return [s for s in ALL if (s in TAIL and body >= 1) or (s in BACK and 0 <= body <= B - 2)
            or (s in FRONT and body <= B - 3)]


def steps_before(step, body, among=ALL):
    def count(steps):
        return sum(s in among for s in steps)
    if isinstance(body, int):
        steps = steps_of(body)
        return sum(count(steps_of(n)) for n in range(-2, body)) + count(steps[:steps.index(step)])
    first = sum(count(steps_of(n)) for n in range(-2, 1)) + count(ALL[:ALL.index(step)])
    return (body - 1) * count(ALL) + first


def same_reader(step):
    return [s for s in ALL if (s in BY_SCALAR) == (step in BY_SCALAR)]


def earlier(count, b, p):
    return (b - p) * (count // 2)


def wait(eng, sem, value):
    if not isinstance(value, int) or value > 0:
        eng.wait_ge(sem, value)


def wait_behind(eng, constant, *waits):
    values = [(s, v if isinstance(v, int) else eng.to_reg(v)) for s, v in waits]
    eng.wait_ge(*constant)
    for s, v in values:
        wait(eng, s, v)


def build(nc, a, out):
    ctx = ExitStack()
    with ctx:
        def sb(name, shape, dt=F32):
            return ctx.enter_context(nc.sbuf_tensor(name, shape, dt))

        def sem(name):
            return ctx.enter_context(nc.semaphore(name))

        ident = sb("ident", [128, 128])
        identb = sb("identb", [128, 128], BF16)
        x0i, x2i = sb("x0i", [128, 2, GP], I32), sb("x2i", [128, 2], I32)
        rows0 = sb("rows0", [128, 2, GP, B * F0])
        table1 = sb("table1", [128, P1 // 128, B * F1])
        rowid = sb("rowid", [128, P1 // 128])
        rows2 = sb("rows2", [128, 2, B * F2])
        wfT = sb("wfT", [EMB, 3, D])
        w0 = sb("w0", [EMB, R0])
        w1T = sb("w1T", [8 * F1, 2, EMB])
        w2T = sb("w2T", [F2, GP, EMB])
        bcol = sb("bcol", [EMB, 3])
        bfrow = sb("bfrow", [1, D])
        ones = sb("ones", [1, 128])
        y1T, y2T = sb("y1T", [EMB, B * G1]), sb("y2T", [EMB, B * G2])
        z1, z2 = sb("z1", [128, B // 2, D]), sb("z2", [128, D])
        fused = sb("fused", [128, B, D])
        patches = sb("patches", [128, 2, 128])
        patchesT = sb("patchesT", [128, NTOK])

        h = sb("h", [128, T, D])
        stats, meanvar, rstd = sb("stats", [128, T, 6]), sb("meanvar", [128, T, 2]), sb("rstd", [128, 2, T])
        negmean = sb("negmean", [128, T])
        minushalf = sb("minushalf", [128, T])
        xn = sb("xn", [128, T, D])
        resid = sb("resid", [128, 2, T, D])
        xT0, xT1 = sb("xT0", [DC, S]), sb("xT1", [DC, S])
        wqk0, wqk1 = sb("wqk0", [DC, 3, 128]), sb("wqk1", [DC, 3, 128])
        wv0, wv1 = sb("wv0", [DC, D]), sb("wv1", [DC, D])
        bqk = sb("bqk", [128, 3])
        qkscale = sb("qkscale", [128, 1])
        bvrow, borow, b2row = sb("bvrow", [128, D]), sb("borow", [128, D]), sb("b2row", [128, D])
        full = sb("full", [128, 2, S])
        rest = sb("rest", [128, 2, S])
        parts = sb("parts", [128, 3, 3, S], BF16)
        stackq = sb("stackq", [SLOTS * DH, 2, H, S], BF16)
        stackk = sb("stackk", [SLOTS * DH, 2, H, S], BF16)
        rows1b = full[:].rearrange("p k n -> p (k n)").rearrange("p (b x) -> p b x", b=B)
        t1T = stackk[:, 1].rearrange("p h n -> p (h n)").bitcast(F32)[:, 0:B * 128].rearrange(
            "p (b t) -> p b t", b=B)
        t2T = stackq[0:F2, 1].rearrange("p h n -> p (h n)").bitcast(F32)[:, 0:2 * B * 128].rearrange(
            "p (j b t) -> p j b t", j=2, b=B)
        v = sb("v", [128, 2, T, D])
        negmax, sums, inv = sb("negmax", [128, 4]), sb("sums", [128, 9, 4]), sb("inv", [128, 9, 4])
        probs = sb("probs", [128, 9, 2, S])
        vs = sb("vs", [128, 3, 4, 32])
        setup = probs[:].rearrange("p r j n -> p (r j n)")
        from1i, from1 = setup[:, 0:P1].bitcast(I32), setup[:, P1:2 * P1]
        pick = setup[:, 2 * P1:6 * P1].rearrange("p (r s t) -> p r s t", r=4, s=P1 // 128)
        ctxT = sb("ctxT", [128, GROUPS, S])
        wo = sb("wo", [128, GROUPS, D])
        h2 = sb("h2", [128, T, D])
        first = sb("first", [128, 1])
        stats2, meanvar2, rstd2 = sb("stats2", [128, T, 6]), sb("meanvar2", [128, T, 2]), sb("rstd2", [128, 2, T])
        negmean2 = sb("negmean2", [128, T])
        xn2 = sb("xn2", [128, T, D])
        xr = sb("xr", [128, T, D])
        xhi, xq = sb("xhi", [128, T, D], BF16), sb("xq", [128, T, D], BF16)
        resid2 = sb("resid2", [128, B * T, D])
        xqT0, xqT1 = sb("xqT0", [DC, B * S], BF16), sb("xqT1", [DC, B * S], BF16)

        early = resid2[:].rearrange("p n d -> p (n d)")
        w1f0, w1f1 = early[0:DC, 0:HID], early[0:DC, HID:2 * HID]
        aw1row, aa2row = early[:, 2 * HID:3 * HID], early[:, 3 * HID:4 * HID]
        w2f = early[:, 4 * HID:4 * HID + MH * D].rearrange("p (m d) -> p m d", m=MH)
        w1q0, w1q1 = sb("w1q0", [DC, HID], BF16), sb("w1q1", [DC, HID], BF16)
        w2q = sb("w2q", [128, MH, D], BF16)
        aw2row, aa1row = sb("aw2row", [128, D]), sb("aa1row", [128, D])
        aw1col, b1col = sb("aw1col", [128, MH]), sb("b1col", [128, MH])
        mean1, mean2 = sb("mean1", [128, 1]), sb("mean2", [128, 1])
        inv1, inv2 = sb("inv1", [128, 1]), sb("inv2", [128, 1])
        top2, low2 = sb("top2", [128, 1]), sb("low2", [128, 1])
        scale1 = sb("scale1", [128, MH])
        scale2 = sb("scale2", [128, D])
        spare = probs[:].rearrange("p r j n -> p (r j) n")
        gelus, rounded = (spare[:, k:k + 4].rearrange("p (r two) n -> p r two n", two=2) for k in (0, 4))
        hhi = sb("hhi", [128, 2, 2, S], BF16)
        hq = sb("hq", [128, 2, MH, S], BF16)
        tail = spare[:, 8:].rearrange("p r n -> p (r n)")[:, 0:3 * T * D].rearrange("p (q t d) -> p q t d", q=3, t=T)
        scaled, result = tail[:, 0], tail[:, 1:3]

        cut = nc.dram_tensor("cut", (2, 3, DH, GROUPS, 2, 4, S), BF16, kind="Internal").ap()

        PS = ctx.enter_context(nc.psum_tensor("PS", [128, 8, 512], F32))
        CTX, SHARED = 6, (7, 4, 5)

        def hidden_bank(p, m):
            return 2 * ((p + m // 2) % 2) + m % 2

        def bank_of(step, body):
            if isinstance(body, int) and body == B:
                return SHARED[0]
            ahead = {"qk0": 0, "qk1": 1, "qk2": 2, "v01": 3} if isinstance(body, int) and body == -2 else {}
            return ahead.get(step, SHARED[ALL.index(step) % 3])

        def reads_before(step, body):
            if isinstance(body, int):
                order = [(n, s) for n in range(-2, B + 1) for s in steps_of(n)]
                order = order[:order.index((body, step))]
                same = [k for k, (n, s) in enumerate(order) if bank_of(s, n) == bank_of(step, body)]
                if not same:
                    return None
                last = order[same[-1]][1]
                return last in BY_SCALAR, sum((s in BY_SCALAR) == (last in BY_SCALAR) for _, s in order[:same[-1] + 1])
            n = ALL.index(step)
            last = ALL[n - 3]
            reader = same_reader(last)
            if n >= 3:
                return last in BY_SCALAR, steps_before(last, body, reader) + 1
            after = sum(s in reader and s not in TAIL for s in ALL[n - 3 + len(ALL) + 1:])
            if last in TAIL:
                after = 0
            return last in BY_SCALAR, steps_before(ALL[0], body, reader) - after

        idx_in, consts_in = sem("idx_in"), sem("consts_in")
        tokw_in, attw_in, scales_in, ffnw_in = sem("tokw_in"), sem("attw_in"), sem("scales_in"), sem("ffnw_in")
        got2, got0, level1_in = sem("got2"), sem("got0"), sem("level1_in")
        pe_set, dve_set, act_set = sem("pe_set"), sem("dve_set"), sem("act_set")
        picks_in, picked = sem("picks_in"), sem("picked")
        prep_chain = sem("prep_chain")
        pool_set, pool_chain = sem("pool_set"), sem("pool_chain")
        fused_in, text_in = sem("fused_in"), sem("text_in")
        patches_in = sem("patches_in")
        bank_full = sem("bank_full")
        vector_read, scalar_read = sem("vector_read"), sem("scalar_read")
        stats_in, meanvar_in, text_used = sem("stats_in"), sem("meanvar_in"), sem("text_used")
        var_in, rstd_in, negmean_in, xn_in = sem("var_in"), sem("rstd_in"), sem("negmean_in"), sem("xn_in")
        part1_in, rest_in, part2_in, part3_in = sem("part1_in"), sem("rest_in"), sem("part2_in"), sem("part3_in")
        cut_in = [sem(f"cut_in{mt}") for mt in range(3)]
        stack_in = [[sem(f"stack_in{p}{half}") for half in range(2)] for p in range(2)]
        scores_in, max_in, exp_in, inv_in, vs_in = (sem("scores_in"), sem("max_in"), sem("exp_in"),
                                                   sem("inv_in"), sem("vs_in"))
        pv_done, ctx_in = sem("pv_done"), sem("ctx_in")
        stats2_in, meanvar2_in = sem("stats2_in"), sem("meanvar2_in")
        var2_in, rstd2_in, negmean2_in, xn2_in = sem("var2_in"), sem("rstd2_in"), sem("negmean2_in"), sem("xn2_in")
        xr_in, xhi_in, xq_in, resid2_in = sem("xr_in"), sem("xhi_in"), sem("xq_in"), sem("resid2_in")
        hid_in, gelu_in, rounded_in, hhi_in, hq_in = (sem("hid_in"), sem("gelu_in"), sem("rounded_in"),
                                                      sem("hhi_in"), sem("hq_in"))
        ffn_in, scaled_in, result_in, stored = sem("ffn_in"), sem("scaled_in"), sem("result_in"), [sem("stored0"), sem("stored1")]

        N_TOKW, N_ATTW, N_SCALES, N_FFNW = 8, 9, 6, 3

        block = ctx.enter_context(nc.Block())

        @block.sync
        def _(sp):
            for dst, src in ((x2i, "idx2"), (x0i, "idx0")):
                sp.dma_start(dst[:], a[src]).then_inc(idx_in, 16)
            sp.dma_start(rowid[:], a["rowid"]).then_inc(level1_in, 16)
            sp.dma_start(table1[:], a["table1"].rearrange("(s p) x -> p s x", p=128)).then_inc(level1_in, 16)
            sp.dma_start(ident[:], a["ident"]).then_inc(consts_in, 16)
            sp.dma_start(patches[:, :, R0:128], a["interp"]).then_inc(consts_in, 16)
            for dst, src in ((w2T, "W2T"), (w1T, "W1T"), (w0, "W0"), (wfT, "WfT")):
                sp.dma_start(dst[:], a[src]).then_inc(tokw_in, 16)
            for n in range(3):
                sp.dma_start(bcol[:, n:n + 1], a[f"b{n}"]).then_inc(tokw_in, 16)
            sp.dma_start(bfrow[:], a["bf"]).then_inc(tokw_in, 16)
            sp.dma_start(h[:, 2, :], a["txt"][0]).then_inc(text_in, 16)
            sp.wait_ge(dve_set, Z2_COPIED)
            for b in range(B):
                sp.dma_start(fused[128 - G2:128, b, :], z2[G2 * b:G2 * (b + 1), :]).then_inc(fused_in, 16)
            sp.wait_ge(dve_set, Z1_COPIED)
            f = fused[R0:R0 + G1, :, :].rearrange("p (q r) d -> p r q d", r=2)
            for r in range(2):
                sp.dma_start(f[:, r], z1[G1 * r:G1 * (r + 1), :, :]).then_inc(fused_in, 16)

            def store_parts(c, p, mt):
                wait_behind(sp, (idx_in, 32), (part1_in, 3 * c + mt + 1),
                            (stack_in[p][min(mt, 1)], earlier(LOADS[min(mt, 1)], c, p)))
                for part, ready in enumerate((part1_in, part2_in, part3_in)):
                    if part > 0:
                        sp.wait_ge(ready, 3 * c + mt + 1)
                    sp.dma_start(cut[p, part, :, mt].rearrange("e k h n -> (k h) e n"), parts[:, mt, part, :]).then_inc(cut_in[mt], 16)

            def load_stacks(c, p, half):
                if half == 0:
                    wait_behind(sp, (idx_in, 32), (scores_in, 2 * PAIRS * (c - 1)), (cut_in[0], 16 * 3 * (c + 1)))
                else:
                    wait_behind(sp, (idx_in, 32), (scores_in, 2 * PAIRS * (c - 1)), (cut_in[1], 16 * 3 * (c + 1)),
                                (cut_in[2], 16 * 3 * (c + 1)))
                g0, n = ((0, 1), (1, 2))[half]
                for s, k in RUNS:
                    rows = slice(DH * s, DH * (s + k))
                    part = PARTS_Q[s]
                    sp.dma_start(stackk[rows, p, 4 * g0:4 * (g0 + n), :],
                                 cut[p, 0:k, :, g0:g0 + n, 1].rearrange("c e g h n -> (c e) g (h n)")).then_inc(stack_in[p][half], 16)
                    if k == 1:
                        sp.dma_start(stackq[rows, p, 4 * g0:4 * (g0 + n), :],
                                     cut[p, part, :, g0:g0 + n, 0].rearrange("e g h n -> e g (h n)")).then_inc(stack_in[p][half], 16)
                        continue
                    for g in range(g0, g0 + n):
                        sp.dma_start(stackq[rows, p, 4 * g:4 * g + 4, :],
                                     cut[p, part:part + 1, :, g, 0].broadcast_to([k, DH, 4, S])).then_inc(stack_in[p][half], 16)

            def stacks(c, p, more=True):
                store_parts(c, p, 0)
                load_stacks(c, p, 0)
                store_parts(c, p, 1)
                if more:
                    text(c + 1)
                store_parts(c, p, 2)
                load_stacks(c, p, 1)

            def text(c):
                wait(sp, text_used, c)
                wait(sp, meanvar_in, c)
                sp.dma_start(h[:, 2, :], a["txt"][c]).then_inc(text_in, 16)

            text(1)
            stacks(0, 0, more=False)
            stacks(1, 1)
            with sp.Fori(1, B // 2 - 1) as i:
                for p in range(2):
                    stacks(2 * i + p, p)
            stacks(B - 2, 0)
            stacks(B - 1, 1, more=False)

            def store(b, p):
                sp.wait_ge(result_in, b + 1)
                sp.dma_start(out[b], result[:, p]).then_inc(stored[p], 16)

            with sp.Fori(0, B // 2) as i:
                for p in range(2):
                    store(2 * i + p, p)
            for p in range(2):
                sp.wait_ge(stored[p], 16 * (B // 2))

        @block.gpsimd
        def _(pool):
            nc.gpsimd.memset(ones[:], 1.0).then_inc(pool_set, 1)
            nc.gpsimd.memset(minushalf[:], -0.5).then_inc(pool_set, 1)
            nc.gpsimd.memset(vs[:], 0.0).then_inc(pool_set, 1)
            nc.gpsimd.memset(first[:], 0.0).then_inc(resid2_in, 1)
            pool.wait_ge(idx_in, 32)

            def gather(dst, table, idx, done):
                nc.gpsimd.indirect_dma_start(dst, None, table, bass.IndirectOffsetOnAxis(ap=idx, axis=0)).then_inc(done, 16)

            for jh in range(2):
                gather(rows2[:, jh, :], a["table2"], x2i[:, jh:jh + 1], got2)
            for t in range(2):
                for j in range(GP):
                    gather(rows0[:, t, j, :], a["table0"], x0i[:, t, j:j + 1], got0)

            def patch_columns(c):
                wait(pool, meanvar_in, c)
                nc.gpsimd.tensor_copy(
                    patches[:, :, 0:R0].rearrange("p t (j c) -> p t j c", c=F0),
                    rows0[:, :, :, bass.ds(F0 * c, F0)]).then_inc(patches_in, 1)

            def layernorm(c, p):
                wait_behind(pool, (pool_set, 3), (meanvar_in, c + 1))
                nc.gpsimd.tensor_scalar(rstd[:, 0, :], meanvar[:, :, 1], 1.0, EPS, ALU.mult, ALU.add).then_inc(var_in, 1)
                nc.gpsimd.tensor_scalar(negmean[:], meanvar[:, :, 0], -1.0, 0.0, ALU.mult, ALU.add).then_inc(negmean_in, 1)
                pool.wait_ge(var_in, c + 1)
                nc.gpsimd.tensor_tensor(out=rstd[:, 1, :], in0=rstd[:, 0, :], in1=minushalf[:], op=ALU.pow).then_inc(rstd_in, 1)
                wait_behind(pool, (pool_set, 3), (rstd_in, c + 1), (negmean_in, c + 1), (part1_in, 3 * c))
                for t in range(T):
                    nc.gpsimd.tensor_scalar(xn[:, t, :], h[:, t, :], negmean[:, t:t + 1], rstd[:, 1, t:t + 1],
                                            ALU.add, ALU.mult).then_inc(xn_in, 1)

            def residual(c, p):
                wait(pool, stats2_in, T * (c - 1))
                nc.gpsimd.tensor_tensor(out=resid[:, p], in0=h[:], in1=borow[:].unsqueeze(1).broadcast_to([128, T, D]),
                                        op=ALU.add).then_inc(text_used, 1)

            def rest_after_part1(c, mt):
                pool.wait_ge(part1_in, 3 * c + mt + 1)
                k = mt % 2
                wait(pool, part3_in, 3 * c + (0, -1, 1)[mt])
                nc.gpsimd.tensor_tensor(out=rest[:, k], in0=full[:, k], in1=parts[:, mt, 0], op=ALU.subtract).then_inc(rest_in, 1)

            def part3(c, mt):
                pool.wait_ge(part2_in, 3 * c + mt + 1)
                k = mt % 2
                nc.gpsimd.tensor_tensor(out=parts[:, mt, 2], in0=rest[:, k], in1=parts[:, mt, 1], op=ALU.subtract).then_inc(part3_in, 1)

            def scale_values(b, p, n):
                g, t, r = n // 3, n % 3, n % 3
                pool.wait_ge(inv_in, BLOCKS * b + n + 1)
                wait(pool, pv_done, BLOCKS * b + n - 2)
                nc.gpsimd.tensor_tensor(
                    out=vs[:, r, :, 0:DH], in0=v[:, p, t, 4 * DH * g:4 * DH * (g + 1)].rearrange("p (h e) -> p h e", e=DH),
                    in1=inv[:, n, :].unsqueeze(2).broadcast_to([128, 4, DH]), op=ALU.mult).then_inc(vs_in, 1)

            def spread2(b):
                wait_behind(pool, (pool_set, 3), (meanvar2_in, b + 1))
                nc.gpsimd.tensor_scalar(rstd2[:, 0, :], meanvar2[:, :, 1], 1.0, EPS, ALU.mult, ALU.add).then_inc(var2_in, 1)
                nc.gpsimd.tensor_scalar(negmean2[:], meanvar2[:, :, 0], -1.0, 0.0, ALU.mult, ALU.add).then_inc(negmean2_in, 1)
                pool.wait_ge(var2_in, b + 1)
                nc.gpsimd.tensor_tensor(out=rstd2[:, 1, :], in0=rstd2[:, 0, :], in1=minushalf[:], op=ALU.pow).then_inc(rstd2_in, 1)

            def normalise2(b, tiles):
                wait_behind(pool, (pool_set, 3), (rstd2_in, b + 1), (negmean2_in, b + 1))
                for t in tiles:
                    nc.gpsimd.tensor_scalar(xn2[:, t, :], h2[:, t, :], negmean2[:, t:t + 1], rstd2[:, 1, t:t + 1],
                                            ALU.add, ALU.mult).then_inc(xn2_in, 1)

            def round2(b):
                wait_behind(pool, (pool_set, 3), (xn2_in, 3 * b + 3))
                nc.gpsimd.tensor_scalar(xr[:], xn2[:], inv1[:], ROUND, ALU.mult, ALU.add).then_inc(xr_in, 1)

            def layernorm2(b):
                spread2(b)
                normalise2(b, range(T))
                round2(b)

            def residual2(b):
                nc.gpsimd.tensor_tensor(out=resid2[:, bass.ds(T * b, T), :], in0=h2[:],
                                        in1=b2row[:].unsqueeze(1).broadcast_to([128, T, D]), op=ALU.add).then_inc(resid2_in, 1)

            pool.wait_ge(got0, 16 * 2 * GP)
            pool.wait_ge(consts_in, 32)
            patch_columns(0)
            pool.wait_ge(attw_in, 16 * N_ATTW)
            layernorm(0, 0)
            residual(0, 0)
            patch_columns(1)
            rest_after_part1(0, 0)
            part3(0, 0)
            rest_after_part1(0, 1)
            rest_after_part1(0, 2)
            part3(0, 1)
            part3(0, 2)
            layernorm(1, 1)

            def body(b, p, front=True, back=True, tail=True):
                c, o, q = b + 1, b - 1, 1 - p
                for k in range(PAIRS):
                    due = [name for name in ON_GPSIMD if ON_GPSIMD[name] == k]
                    if k % 2 == VALUES_LAG % 2:
                        if k >= VALUES_LAG:
                            scale_values(b, p, (k - VALUES_LAG) // 2)
                        elif tail:
                            scale_values(o, q, BLOCKS + (k - VALUES_LAG) // 2)
                    if "patches" in due and front:
                        patch_columns(b + 2)
                    if "layernorm" in due and front:
                        layernorm(b + 2, p)
                    if "residual" in due and back:
                        residual(c, q)
                    if "layernorm2" in due and tail:
                        layernorm2(o)
                    if "rest0" in due and back:
                        rest_after_part1(c, 0)
                    if "part30" in due and back:
                        part3(c, 0)
                    if "rest1" in due and back:
                        rest_after_part1(c, 1)
                    if "rest2" in due and back:
                        rest_after_part1(c, 2)
                    if "part31" in due and back:
                        part3(c, 1)
                    if "part32" in due and back:
                        part3(c, 2)
                    if "residual2" in due and tail:
                        residual2(o)

            pool.wait_ge(dve_set, WEIGHTS_READY)
            body(0, 0, tail=False)
            with pool.Fori(0, (B - 4) // 2) as i:
                body(2 * i + 1, 1)
                body(2 * i + 2, 0)
            body(B - 3, 1)
            body(B - 2, 0, front=False)
            body(B - 1, 1, front=False, back=False)
            for n in range((PAIRS - VALUES_LAG + 1) // 2, BLOCKS):
                scale_values(B - 1, 1, n)

            def round_hidden(b, p, j):
                r = (p + j) % 2
                wait_behind(pool, (pool_set, 3), (gelu_in, MH * b + 2 * j + 2), (hhi_in, MP * b + j - 1))
                nc.gpsimd.tensor_scalar(rounded[:, r], gelus[:, r], inv2[:], ROUND, ALU.mult, ALU.add).then_inc(rounded_in, 1)

            round_hidden(0, 0, 0)
            round_hidden(0, 0, 1)
            spread2(B - 1)
            round_hidden(0, 0, 2)
            normalise2(B - 1, (0,))
            round_hidden(1, 1, 0)
            normalise2(B - 1, (1, 2))
            round_hidden(1, 1, 1)
            round2(B - 1)
            round_hidden(1, 1, 2)
            residual2(B - 1)
            with pool.Fori(1, B // 2) as i:
                for p in range(2):
                    for j in range(MP):
                        round_hidden(2 * i + p, p, j)

        @block.scalar
        def _(act):
            act.dma_start(from1i, a["idx1"].broadcast_to([128, P1])).then_inc(level1_in, 16)
            for dst, src in ((aw1row, "aw1row"), (aw2row, "aw2row"), (aa1row, "aa1row"), (aa2row, "aa2row"),
                             (aw1col, "aw1col"), (b1col, "b1col")):
                act.dma_start(dst[:], a[src]).then_inc(scales_in, 16)
            for dst, src in ((wqk0, "wqk0"), (wqk1, "wqk1"), (wv0, "wv0"), (wv1, "wv1"), (bqk, "bqk"), (wo, "wo"),
                             (bvrow, "bvrow"), (borow, "borow"), (b2row, "b2row")):
                act.dma_start(dst[:], a[src]).then_inc(attw_in, 16)
            for dst, src in ((w1f0, "w1f0"), (w1f1, "w1f1"), (w2f, "w2f")):
                act.dma_start(dst[:], a[src]).then_inc(ffnw_in, 16)

            def full_bank(step, body):
                act.wait_ge(bank_full, steps_before(step, body) + 1)

            def read_tokens(c, body):
                full_bank("tokens", body)
                wait(act, text_used, c)
                nc.scalar.copy(h[:, 0:2, :], PS[:, bank_of("tokens", body), 0:2 * D].rearrange("p (t d) -> p t d", t=2)).then_inc(scalar_read, 1)

            def read_x(part, body):
                full_bank(f"turn_x{part}", body)
                nc.scalar.copy((xT0, xT1)[part][:], PS[0:DC, bank_of(f"turn_x{part}", body), 0:S]).then_inc(scalar_read, 1)

            def read_context(b, g, tail):
                act.wait_ge(pv_done, BLOCKS * b + 3 * g + 3)
                if g == 0 and tail:
                    act.wait_ge(bank_full, steps_before("out2", b) + 1)
                nc.scalar.copy(ctxT[:, g, :], PS[:, CTX, 0:S]).then_inc(ctx_in, 1)

            def body(b, front=True, back=True, tail=True):
                for k in range(PAIRS):
                    if k % 2 == 1:
                        wait(act, pv_done, BLOCKS * b + (k - 9) // 2 + 1)
                    for j in range(2):
                        u = 2 * k + j
                        act.wait_ge(max_in, 2 * PAIRS * b + u + 1)
                        nc.scalar.activation(probs[:, k % 9, j, :], PS[:, u % 4, 0:S], ACT.Exp, bias=negmax[:, u % 4:u % 4 + 1],
                                             accum_out=sums[:, k // 2, u % 4:u % 4 + 1]).then_inc(exp_in, 1)
                    if k == ON_SCALAR["tokens"] and front:
                        read_tokens(b + 2, b)
                    group, late = divmod(k - ON_SCALAR["context"], 6)
                    if late == 0 and group >= 0:
                        read_context(b, group, tail)
                    elif late == 0 and tail:
                        read_context(b - 1, GROUPS + group, True)
                    for part in range(2):
                        if k == ON_SCALAR[f"turn_x{part}"] and back:
                            read_x(part, b)

            def picked_rows(n):
                act.wait_ge(picked, 4 * n + 4)
                nc.scalar.copy(rows1b[:, :, 4 * F1 * n:4 * F1 * (n + 1)].rearrange("p b (j f) -> p j b f", j=4),
                               PS[:, 6 + n, 0:4 * B * F1].rearrange("p (j b f) -> p j b f", j=4, b=B)).then_inc(act_set, 1)

            for n in range(4):
                act.wait_ge(pe_set, n + 1)
                nc.scalar.copy(t2T[:, n // 2, 4 * (n % 2):4 * (n % 2) + 4, :],
                               PS[0:F2, n, :].rearrange("p (b t) -> p b t", b=4)).then_inc(act_set, 1)
            picked_rows(0)
            act.wait_ge(dve_set, 3)
            nc.scalar.copy(fused[0:R0, :, :], PS[0:R0, 5, D:2 * D].unsqueeze(1).broadcast_to([R0, B, D])).then_inc(act_set, 1)
            picked_rows(1)
            for n in range(2):
                act.wait_ge(pe_set, 8 + n)
                nc.scalar.copy(t1T[:, 4 * n:4 * n + 4, :],
                               PS[0:8 * F1, n, :].rearrange("p (b t) -> p b t", b=4)).then_inc(act_set, 1)

            read_tokens(0, -2)
            read_x(0, -2)
            read_x(1, -2)
            read_tokens(1, -1)
            body(0, tail=False)
            with act.Fori(1, B - 2) as i:
                body(i)
            body(B - 2, front=False)
            body(B - 1, front=False, back=False)
            read_context(B - 1, 2, True)

            def gelu(b, p, m):
                if m % 2 == 0:
                    wait(act, rounded_in, MP * b + m // 2 - 1)
                act.wait_ge(hid_in, MH * b + m + 1)
                nc.scalar.activation(gelus[:, (p + m // 2) % 2, m % 2], PS[:, hidden_bank(p, m), 0:S], ACT.Gelu, bias=b1col[:, m:m + 1],
                                     scale=scale1[:, m:m + 1]).then_inc(gelu_in, 1)

            for b in range(2):
                for m in range(MH):
                    gelu(b, b, m)
            with act.Fori(1, B // 2) as i:
                for p in range(2):
                    for m in range(MH):
                        gelu(2 * i + p, p, m)

        @block.vector
        def _(dve):
            chain = [0]

            def link(instruction):
                chain[0] += 1
                instruction.then_inc(prep_chain, 1)
                dve.wait_ge(prep_chain, chain[0])

            def pick_patch(j):
                wait(dve, picked, j - 3)
                nc.vector.tensor_tensor(out=pick[:, j % 4], in0=from1[:, 128 * j:128 * (j + 1)].unsqueeze(1).broadcast_to([128, P1 // 128, 128]),
                                        in1=rowid[:].unsqueeze(2).broadcast_to([128, P1 // 128, 128]),
                                        op=ALU.is_equal).then_inc(picks_in, 1)

            dve.wait_ge(level1_in, 48)
            link(nc.vector.tensor_copy(from1, from1i))
            for j in range(4):
                pick_patch(j)
            dve.wait_ge(consts_in, 32)
            nc.vector.tensor_copy(identb[:], ident[:]).then_inc(dve_set, 1)
            link(nc.vector.memset(qkscale[:], 1.0))
            link(nc.vector.memset(qkscale[0:64, :], DH ** -0.5))
            pick_patch(4)
            pick_patch(5)
            dve.wait_ge(scales_in, 16 * N_SCALES)
            link(nc.vector.tensor_reduce(out=mean1[:], in_=aa1row[:], axis=AX.X, op=ALU.add))
            link(nc.vector.tensor_scalar(mean1[:], mean1[:], 1.0 / D, None, ALU.mult))
            link(nc.vector.tensor_reduce(out=mean2[:], in_=aa2row, axis=AX.X, op=ALU.add))
            link(nc.vector.tensor_scalar(mean2[:], mean2[:], 1.0 / HID, None, ALU.mult))
            link(nc.vector.reciprocal(inv1[:], mean1[:]))
            link(nc.vector.reciprocal(inv2[:], mean2[:]))
            link(nc.vector.tensor_scalar(scale1[:], aw1col[:], mean1[:], None, ALU.mult))
            link(nc.vector.tensor_scalar(scale2[:], aw2row[:], mean2[:], None, ALU.mult))
            link(nc.vector.tensor_scalar(top2[:], inv2[:], CLIP, QP, ALU.mult, ALU.min))
            link(nc.vector.tensor_scalar(top2[:], top2[:], ROUND, ROUND, ALU.add, ALU.subtract))
            link(nc.vector.tensor_scalar(low2[:], inv2[:], -CLIP, QN, ALU.mult, ALU.max))
            link(nc.vector.tensor_scalar(low2[:], low2[:], ROUND, ROUND, ALU.add, ALU.subtract))
            link(nc.vector.reciprocal(aw1row, aw1row))
            dve.wait_ge(pe_set, 5)
            dve.wait_ge(tokw_in, 16 * N_TOKW)
            nc.vector.tensor_scalar(y2T[:], PS[0:EMB, 4, 0:B * G2], bcol[:, 2:3], None, ALU.add).then_inc(dve_set, 1)
            pick_patch(6)
            pick_patch(7)
            dve.wait_ge(pe_set, 7)
            nc.vector.tensor_copy(z2[:], PS[:, 5, 0:D]).then_inc(dve_set, 1)
            link(nc.vector.reciprocal(aw2row[:], aw2row[:]))
            dve.wait_ge(pe_set, 10)
            nc.vector.tensor_scalar(y1T[:], PS[0:EMB, 2, :], bcol[:, 1:2], None, ALU.add).then_inc(dve_set, 1)
            for n in range(2):
                dve.wait_ge(pe_set, 11 + n)
                nc.vector.tensor_copy(z1[:, 2 * n:2 * n + 2, :],
                                      PS[:, 3 + n, 0:2 * D].rearrange("p (q d) -> p q d", q=2)).then_inc(dve_set, 1)

            def whole_weights(w, wq, r):
                link(nc.vector.tensor_tensor(out=w, in0=w, in1=r, op=ALU.mult))
                link(nc.vector.tensor_scalar(w, w, QN, QP, ALU.max, ALU.min))
                link(nc.vector.tensor_scalar(wq, w, ROUND, ROUND, ALU.add, ALU.subtract))

            def full_bank(step, body):
                dve.wait_ge(bank_full, steps_before(step, body) + 1)

            def own_read(step, body):
                dve.wait_ge(vector_read, steps_before(step, body, same_reader(step)) + 1)

            def read_patches(c, p, body):
                full_bank("turn_patches", body)
                nc.vector.tensor_copy(patchesT[:], PS[:, bank_of("turn_patches", body), 0:NTOK]).then_inc(vector_read, 1)

            def token_stats(c, body):
                dve.wait_ge(scalar_read, steps_before("tokens", body, BY_SCALAR) + 1)
                dve.wait_ge(text_in, 16 * c + 16)
                for t in range(T):
                    nc.vector.bn_stats(stats[:, t, :], h[:, t, :]).then_inc(stats_in, 1)

            def token_stats_ready(c):
                dve.wait_ge(stats_in, T * c + T)

            def token_meanvar(c):
                for t in range(T):
                    done = nc.vector.bn_aggr(meanvar[:, t, :], stats[:, t, :])
                done.then_inc(meanvar_in, 1)

            def read_qk(c, mt, body):
                full_bank(f"qk{mt}", body)
                k = mt % 2
                wait(dve, rest_in, 3 * c + (0, -1, 1)[mt])
                nc.vector.tensor_scalar(full[:, k], PS[:, bank_of(f"qk{mt}", body), 0:S], bqk[:, mt:mt + 1], qkscale[:],
                                        ALU.add, ALU.mult).then_inc(vector_read, 1)

            def part1(c, mt, body):
                own_read(f"qk{mt}", body)
                wait(dve, cut_in[mt], 16 * 3 * c)
                nc.vector.tensor_copy(parts[:, mt, 0], full[:, mt % 2]).then_inc(part1_in, 1)

            def part2(c, mt):
                dve.wait_ge(rest_in, 3 * c + mt + 1)
                nc.vector.tensor_copy(parts[:, mt, 1], rest[:, mt % 2]).then_inc(part2_in, 1)

            def read_v(c, p, step, body):
                full_bank(step, body)
                wait(dve, vs_in, BLOCKS * (c - 1))
                t, n = (0, 2) if step == "v01" else (2, 1)
                nc.vector.tensor_tensor(out=v[:, p, t:t + n, :], in0=PS[:, bank_of(step, body), 0:n * D].rearrange("p (t d) -> p t d", t=n),
                                        in1=bvrow[:].unsqueeze(1).broadcast_to([128, n, D]), op=ALU.add).then_inc(vector_read, 1)

            def negative_max(b, n):
                for u in (2 * n, 2 * n + 1):
                    dve.wait_ge(scores_in, 2 * PAIRS * b + u + 1)
                    nc.vector.tensor_reduce(out=negmax[:, u % 4:u % 4 + 1], in_=PS[:, u % 4, 0:S], axis=AX.X, op=ALU.max,
                                            negate=True).then_inc(max_in, 1)

            def inverse_sums(b, n):
                dve.wait_ge(exp_in, 2 * PAIRS * b + 4 * n + 4)
                nc.vector.reciprocal(inv[:, n, :], sums[:, n, :]).then_inc(inv_in, 1)

            def read_out(b, p, step, body):
                full_bank(step, body)
                dve.wait_ge(resid2_in, b + 1)
                t, n = (0, 2) if step == "out01" else (2, 1)
                nc.vector.tensor_tensor(out=h2[:, t:t + n, :], in0=PS[:, bank_of(step, body), 0:n * D].rearrange("p (t d) -> p t d", t=n),
                                        in1=resid[:, p, t:t + n, :], op=ALU.add).then_inc(vector_read, 1)

            def out_stats(b, body):
                own_read("out2", body)
                for t in range(T):
                    nc.vector.bn_stats(stats2[:, t, :], h2[:, t, :]).then_inc(stats2_in, 1)

            def out_stats_ready(b):
                dve.wait_ge(stats2_in, T * b + T)

            def out_meanvar(b):
                for t in range(T):
                    done = nc.vector.bn_aggr(meanvar2[:, t, :], stats2[:, t, :])
                done.then_inc(meanvar2_in, 1)

            def quantise(b):
                dve.wait_ge(xr_in, b + 1)
                nc.vector.tensor_scalar(xhi[:], xr[:], ROUND, QP, ALU.subtract, ALU.min).then_inc(xhi_in, 1)
                dve.wait_ge(xhi_in, b + 1)
                nc.vector.tensor_scalar(xq[:], xhi[:], QN, None, ALU.max).then_inc(xq_in, 1)

            def read_xq(b, body):
                full_bank("turn_xq", body)
                turned = PS[:, bank_of("turn_xq", body), :].bitcast(BF16)
                nc.vector.tensor_copy(xqT0[:, bass.ds(S * b, S)], turned[0:DC, 0:S])
                nc.vector.tensor_copy(xqT1[:, bass.ds(S * b, S)], turned[0:DC, 512:512 + S]).then_inc(vector_read, 1)

            read_patches(0, 0, -2)
            dve.wait_ge(ffnw_in, 16 * N_FFNW)
            whole_weights(w1f0, w1q0[:], aw1row[0:DC])
            token_stats(0, -2)
            token_stats_ready(0)
            token_meanvar(0)
            whole_weights(w1f1, w1q1[:], aw1row[0:DC])
            whole_weights(w2f, w2q[:], aw2row[:].unsqueeze(1).broadcast_to([128, MH, D]))
            nc.vector.memset(h2[:, 0, 0:1], 0.0).then_inc(dve_set, 1)
            for mt in range(3):
                read_qk(0, mt, -2)
                part1(0, mt, -2)
                if mt != 1:
                    part2(0, mt // 2)
            part2(0, 2)
            read_v(0, 0, "v01", -2)
            read_v(0, 0, "v2", -2)
            read_patches(1, 1, -1)
            token_stats(1, -1)
            token_stats_ready(1)
            token_meanvar(1)

            def body(b, p, front=True, back=True, tail=True):
                c, o, q = b + 1, b - 1, 1 - p
                for k in range(PAIRS):
                    due = [name for name in ON_VECTOR if ON_VECTOR[name] == k]
                    if "token_meanvar" in due and front:
                        token_stats_ready(b + 2)
                    if "out_meanvar" in due and tail:
                        out_stats_ready(o)
                    negative_max(b, k)
                    if "token_meanvar" in due and front:
                        token_meanvar(b + 2)
                    if "out_meanvar" in due and tail:
                        out_meanvar(o)
                    if k % 2 == INV_LAG % 2:
                        if k >= INV_LAG:
                            inverse_sums(b, (k - INV_LAG) // 2)
                        elif tail:
                            inverse_sums(o, BLOCKS + (k - INV_LAG) // 2)
                    if back:
                        for mt in range(3):
                            if f"part2{mt}" in due:
                                part2(c, mt)
                            if f"qk{mt}" in due:
                                read_qk(c, mt, b)
                                part1(c, mt, b)
                        for step in ("v01", "v2"):
                            if step in due:
                                read_v(c, q, step, b)
                    if tail:
                        for step in ("out01", "out2"):
                            if step in due:
                                read_out(o, q, step, b)
                        if "out2" in due:
                            out_stats(o, b)
                        if "quantise" in due:
                            quantise(o)
                        if "turn_xq" in due:
                            read_xq(o, b)
                    if front:
                        if "turn_patches" in due:
                            read_patches(b + 2, p, b)
                        if "token_stats" in due:
                            token_stats(b + 2, b)

            body(0, 0, tail=False)
            with dve.Fori(0, (B - 4) // 2) as i:
                body(2 * i + 1, 1)
                body(2 * i + 2, 0)
            body(B - 3, 1)
            body(B - 2, 0, front=False)
            body(B - 1, 1, front=False, back=False)
            for n in range((PAIRS - INV_LAG + 1) // 2, BLOCKS):
                inverse_sums(B - 1, n)
            def clip_above(b, p, j):
                r = (p + j) % 2
                dve.wait_ge(rounded_in, MP * b + j + 1)
                wait(dve, hq_in, MP * b + j - 1)
                nc.vector.tensor_scalar(hhi[:, r], rounded[:, r], ROUND, top2[:], ALU.subtract, ALU.min).then_inc(hhi_in, 1)

            def clip_below(b, p, j):
                dve.wait_ge(hhi_in, MP * b + j + 1)
                wait(dve, ffn_in, 2 * (b - 1))
                nc.vector.tensor_scalar(hq[:, p, 2 * j:2 * j + 2], hhi[:, (p + j) % 2], low2[:], None, ALU.max).then_inc(hq_in, 1)

            def finish(b, p):
                for k, (t, n) in enumerate(((0, 2), (2, 1))):
                    dve.wait_ge(ffn_in, 2 * b + k + 1)
                    wait(dve, result_in, b)
                    nc.vector.tensor_tensor(
                        out=scaled[:, t:t + n, :], in0=PS[:, 4 + 2 * p + k, 0:n * D].rearrange("p (t d) -> p t d", t=n),
                        in1=scale2[:].unsqueeze(1).broadcast_to([128, n, D]), op=ALU.mult).then_inc(scaled_in, 1)
                dve.wait_ge(scaled_in, 2 * b + 2)
                dve.wait_ge(resid2_in, b + 2)
                wait(dve, stored[p], earlier(16, b, p))
                nc.vector.tensor_tensor(out=result[:, p], in0=scaled[:], in1=resid2[:, bass.ds(T * b, T), :],
                                        op=ALU.add).then_inc(result_in, 1)

            def ffn(b, p, last=True, turn=False):
                for j in range(MP):
                    clip_above(b, p, j)
                    if j > 0:
                        clip_below(b, p, j - 1)
                    if turn and j == 0:
                        read_xq(B - 1, B)
                    if last and j == 0:
                        finish(b - 2, p)
                clip_below(b, p, MP - 1)

            read_out(B - 1, 1, "out01", B)
            read_out(B - 1, 1, "out2", B)
            out_stats(B - 1, B)
            out_stats_ready(B - 1)
            for j in range(MP):
                clip_above(0, 0, j)
                if j > 0:
                    clip_below(0, 0, j - 1)
                if j == 0:
                    out_meanvar(B - 1)
            clip_below(0, 0, MP - 1)
            ffn(1, 1, last=False)
            quantise(B - 1)
            ffn(2, 0, turn=True)
            ffn(3, 1)
            with dve.Fori(2, B // 2) as i:
                ffn(2 * i, 0)
                ffn(2 * i + 1, 1)
            finish(B - 2, 0)
            finish(B - 1, 1)

        @block.tensor
        def _(pe):
            mm = nc.tensor.matmul
            def pick_rows(j):
                pe.wait_ge(picks_in, j + 1)
                for n in range(P1 // 128):
                    done = mm(PS[:, 6 + j // 4, B * F1 * (j % 4):B * F1 * (j % 4 + 1)], pick[:, j % 4, n, :], table1[:, n, :],
                              start=(n == 0), stop=(n == P1 // 128 - 1))
                done.then_inc(picked, 1)

            pick_rows(0)
            pick_rows(1)
            pe.wait_ge(consts_in, 32)
            pe.wait_ge(got2, 32)
            for n in range(4):
                for k in range(4):
                    jh, b = n // 2, 4 * (n % 2) + k
                    done = nc.tensor.transpose(PS[0:F2, n, 128 * k:128 * (k + 1)], rows2[:, jh, F2 * b:F2 * (b + 1)], ident[:])
                done.then_inc(pe_set, 1)
            pick_rows(2)
            pick_rows(3)
            pe.wait_ge(tokw_in, 16 * N_TOKW)
            pe.wait_ge(act_set, 4)
            for j in range(GP):
                jh, jl = j // 8, j % 8
                done = mm(PS[0:EMB, 4, 0:B * G2], w2T[:, j, :], t2T[:, jh, :, G2 * jl:G2 * (jl + 1)], start=(j == 0), stop=(j == GP - 1))
            done.then_inc(pe_set, 1)
            pick_rows(4)
            pick_rows(5)
            pe.wait_ge(dve_set, 2)
            pe.wait_ge(pool_set, 3)
            mm(PS[:, 5, 0:D], y2T[:], wfT[:, 2, :], start=True, stop=False)
            mm(PS[:, 5, 0:D], bcol[:, 0:1].broadcast_to([EMB, 128]), wfT[:, 0, :], start=False, stop=False)
            mm(PS[:, 5, 0:D], ones[:], bfrow[:], start=False, stop=True).then_inc(pe_set, 1)
            mm(PS[0:R0, 5, D:2 * D], w0[:], wfT[:, 0, :], start=True, stop=True).then_inc(pe_set, 1)
            pick_rows(6)
            pick_rows(7)
            pe.wait_ge(act_set, 7)
            for n in range(2):
                for k in range(4):
                    b = 4 * n + k
                    done = nc.tensor.transpose(PS[0:8 * F1, n, 128 * k:128 * (k + 1)], rows1b[:, b, :], ident[:])
                done.then_inc(pe_set, 1)
            pe.wait_ge(act_set, 9)
            for jh in range(2):
                done = mm(PS[0:EMB, 2, :], w1T[:, jh, :], t1T[:, :, G1 * jh:G1 * (jh + 1)], start=(jh == 0), stop=(jh == 1))
            done.then_inc(pe_set, 1)
            pe.wait_ge(dve_set, 4)
            for n in range(2):
                for k in range(2):
                    q = 2 * n + k
                    done = mm(PS[:, 3 + n, D * k:D * (k + 1)], y1T[:, 128 * q:128 * (q + 1)], wfT[:, 1, :], start=True, stop=True)
                done.then_inc(pe_set, 1)
            pe.wait_ge(attw_in, 16 * N_ATTW)

            def bank_free(step, body):
                before = reads_before(step, body)
                if before is not None:
                    by_scalar, count = before
                    pe.wait_ge(scalar_read if by_scalar else vector_read, count)

            def turn_patches(c, p, body):
                bank_free("turn_patches", body)
                pe.wait_ge(patches_in, c + 1)
                for t in range(2):
                    done = nc.tensor.transpose(PS[:, bank_of("turn_patches", body), 128 * t:128 * (t + 1)], patches[:, t, :], ident[:])
                done.then_inc(bank_full, 1)

            def tokens(c, p, body):
                bank_free("tokens", body)
                pe.wait_ge(vector_read, steps_before("turn_patches", body, same_reader("turn_patches")) + 1)
                for t in range(2):
                    done = mm(PS[:, bank_of("tokens", body), D * t:D * (t + 1)], patchesT[:, 128 * t:128 * (t + 1)],
                              fused[:, bass.ds(c, 1), :].rearrange("p o d -> p (o d)"), start=True, stop=True)
                done.then_inc(bank_full, 1)

            def turn_x(c, p, body, part):
                bank_free(f"turn_x{part}", body)
                pe.wait_ge(xn_in, T * c + T)
                for t in range(T):
                    done = nc.tensor.transpose(PS[0:DC, bank_of(f"turn_x{part}", body), 128 * t:128 * (t + 1)], xn[:, t, DC * part:DC * (part + 1)], ident[:])
                done.then_inc(bank_full, 1)

            def qk(c, p, body, mt):
                bank_free(f"qk{mt}", body)
                if mt == 0:
                    pe.wait_ge(scalar_read, steps_before("turn_x1", body, BY_SCALAR) + 1)
                bank = bank_of(f"qk{mt}", body)
                mm(PS[:, bank, 0:S], wqk0[:, mt, :], xT0[:], start=True, stop=False)
                mm(PS[:, bank, 0:S], wqk1[:, mt, :], xT1[:], start=False, stop=True).then_inc(bank_full, 1)

            def values(c, p, body, tiles, step):
                bank_free(step, body)
                bank = bank_of(step, body)
                for k, t in enumerate(tiles):
                    mm(PS[:, bank, D * k:D * (k + 1)], xT0[:, 128 * t:128 * (t + 1)], wv0[:], start=True, stop=False)
                    done = mm(PS[:, bank, D * k:D * (k + 1)], xT1[:, 128 * t:128 * (t + 1)], wv1[:], start=False, stop=True)
                done.then_inc(bank_full, 1)

            def project_out(b, body, tiles, step):
                bank_free(step, body)
                pe.wait_ge(ctx_in, GROUPS * b + GROUPS)
                for k, t in enumerate(tiles):
                    for g in range(GROUPS):
                        done = mm(PS[:, bank_of(step, body), D * k:D * (k + 1)], ctxT[:, g, 128 * t:128 * (t + 1)], wo[:, g, :],
                                  start=(g == 0), stop=(g == GROUPS - 1))
                done.then_inc(bank_full, 1)

            def turn_xq(b, body):
                bank_free("turn_xq", body)
                pe.wait_ge(xq_in, b + 1)
                turned = PS[:, bank_of("turn_xq", body), :].bitcast(BF16)
                for t in range(T):
                    nc.tensor.transpose(turned[0:DC, 128 * t:128 * (t + 1)], xq[:, t, 0:DC], identb[:])
                for t in range(T):
                    done = nc.tensor.transpose(turned[0:DC, 512 + 128 * t:512 + 128 * (t + 1)], xq[:, t, DC:D], identb[:])
                done.then_inc(bank_full, 1)

            def run(step, b, p, body):
                if step == "turn_patches":
                    turn_patches(b, p, body)
                elif step == "tokens":
                    tokens(b, p, body)
                elif step in ("turn_x0", "turn_x1"):
                    turn_x(b, p, body, int(step[-1]))
                elif step in ("qk0", "qk1", "qk2"):
                    qk(b, p, body, int(step[-1]))
                elif step in ("v01", "v2"):
                    values(b, p, body, (0, 1) if step == "v01" else (2,), step)
                elif step in ("out01", "out2"):
                    project_out(b, body, (0, 1) if step == "out01" else (2,), step)
                else:
                    turn_xq(b, body)

            def scores(b, p, n):
                g, t, k = n // 6, (n % 6) // 2, n % 2
                if n in (0, 6):
                    pe.wait_ge(stack_in[p][n // 6], earlier(LOADS[n // 6], b, p) + LOADS[n // 6])
                for j in range(2):
                    head, u = 4 * g + 2 * k + j, 2 * n + j
                    wait(pe, exp_in, 2 * PAIRS * b + u - 3)
                    mm(PS[:, u % 4, 0:S], stackk[:, p, head, 128 * t:128 * (t + 1)], stackq[:, p, head, :],
                       start=True, stop=True).then_inc(scores_in, 1)

            def context(b, n):
                g, t, r = n // 3, n % 3, n % 3
                pe.wait_ge(vs_in, BLOCKS * b + n + 1)
                if t == 0:
                    wait(pe, ctx_in, GROUPS * b + g)
                for j in range(4):
                    done = mm(PS[32 * j:32 * (j + 1), CTX, 0:S], vs[:, r, j, :], probs[:, (2 * n + j // 2) % 9, j % 2, :],
                              start=(t == 0), stop=(t == 2))
                done.then_inc(pv_done, 1)

            pe.wait_ge(dve_set, Z1_COPIED)
            pe.wait_ge(act_set, 9)
            for step in steps_of(-2):
                if step == "tokens":
                    pe.wait_ge(fused_in, 16 * (B + 2))
                    pe.wait_ge(act_set, 6)
                run(step, 0, 0, -2)
            for step in steps_of(-1):
                run(step, 1, 1, -1)

            def body(b, p, front=True, back=True, tail=True):
                for k in range(PAIRS):
                    scores(b, p, k)
                    for step in ALL:
                        if ON_TENSOR[step] == k:
                            if step in FRONT and front:
                                run(step, b + 2, p, b)
                            elif step in BACK and back:
                                run(step, b + 1, 1 - p, b)
                            elif step in TAIL and tail:
                                run(step, b - 1, 1 - p, b)
                    if k % 2 == CONTEXT_LAG % 2:
                        if k >= CONTEXT_LAG:
                            context(b, (k - CONTEXT_LAG) // 2)
                        elif tail:
                            context(b - 1, BLOCKS + (k - CONTEXT_LAG) // 2)

            pe.wait_ge(vector_read, steps_before("v2", -2, same_reader("v2")) + 1)
            body(0, 0, tail=False)
            with pe.Fori(0, (B - 4) // 2) as i:
                body(2 * i + 1, 1)
                body(2 * i + 2, 0)
            body(B - 3, 1)
            body(B - 2, 0, front=False)
            body(B - 1, 1, front=False, back=False)
            for n in range((PAIRS - CONTEXT_LAG + 1) // 2, BLOCKS):
                context(B - 1, n)
            def hidden(b, p, m):
                wait(pe, gelu_in, MH * b + m - 3)
                bank = hidden_bank(p, m)
                mm(PS[:, bank, 0:S], w1q0[:, 128 * m:128 * (m + 1)], xqT0[:, bass.ds(S * b, S)], start=True, stop=False)
                mm(PS[:, bank, 0:S], w1q1[:, 128 * m:128 * (m + 1)], xqT1[:, bass.ds(S * b, S)], start=False, stop=True).then_inc(hid_in, 1)

            def back(b, p, t):
                pe.wait_ge(hq_in, MP * b + MP)
                for m in range(MH):
                    done = mm(PS[:, 4 + 2 * p + t // 2, D * (t % 2):D * (t % 2 + 1)], hq[:, p, m, 128 * t:128 * (t + 1)],
                              w2q[:, m, :], start=(m == 0), stop=(m == MH - 1))
                if t > 0:
                    done.then_inc(ffn_in, 1)

            pe.wait_ge(dve_set, WEIGHTS_READY)
            pe.wait_ge(exp_in, 2 * PAIRS * B)
            for m in range(MH):
                if m == 4:
                    run("out01", B - 1, 1, B)
                    run("out2", B - 1, 1, B)
                hidden(0, 0, m)

            def ffn(b, p, turn=False):
                for m in range(MH):
                    hidden(b, p, m)
                    if turn and m == 1:
                        run("turn_xq", B - 1, 1, B)
                    if m == MH - 2:
                        if turn:
                            pe.wait_ge(vector_read, steps_before("turn_xq", B, same_reader("turn_xq")) + 1)
                        back(b - 1, 1 - p, 0)
                for t in range(1, T):
                    back(b - 1, 1 - p, t)

            ffn(1, 1)
            ffn(2, 0, turn=True)
            ffn(3, 1)
            with pe.Fori(2, B // 2) as i:
                ffn(2 * i, 0)
                ffn(2 * i + 1, 1)
            for t in range(T):
                back(B - 1, 1, t)


Z2_COPIED, Z1_COPIED, WEIGHTS_READY = 3, 6, 7


def interpolation(n_in, n_out):
    pos = np.clip((np.arange(n_out, dtype=np.float32) + 0.5) * (n_in / n_out) - 0.5, 0.0, n_in - 1)
    i0 = np.floor(pos).astype(np.int32)
    i1 = np.minimum(i0 + 1, n_in - 1)
    w = (pos - i0).astype(np.float32)
    m = np.zeros((n_out, n_in), np.float32)
    m[np.arange(n_out), i0] += 1.0 - w
    m[np.arange(n_out), i1] += w
    return m


def kernel(**inputs):
    import concourse.bacc as bacc
    from concourse.bass_utils import run_bass_kernel_spmd

    i = {k: np.asarray(v) for k, v in inputs.items()}
    tok = {k[len("L0_tok_"):]: v for k, v in i.items() if k.startswith("L0_tok_")}
    att = {k[len("L0_attn_"):]: v for k, v in i.items() if k.startswith("L0_attn_")}
    ffn = {k[len("L0_ffn_"):]: v for k, v in i.items() if k.startswith("L0_ffn_")}
    x = i["x"]

    def table(p):
        n = IMG // p
        t = x.reshape(B, CH, n, p, n, p).transpose(2, 4, 0, 3, 5, 1)
        return t.reshape(n * n, B * p * p * CH)

    def heads_first(w):
        return w.transpose(1, 0, 2).reshape(D, H * DH)

    def rows(r):
        return np.broadcast_to(r.reshape(1, -1), (128, r.size))

    wq, wk, wv = (heads_first(att[k]) for k in ("Wq", "Wk", "Wv"))
    bq, bk = att["bq"].reshape(-1), att["bk"].reshape(-1)
    wqk = np.stack([wq.reshape(D, GROUPS, 64), wk.reshape(D, GROUPS, 64)], 2).reshape(D, GROUPS, 128)
    bqk = np.stack([bq.reshape(GROUPS, 64), bk.reshape(GROUPS, 64)], 1).reshape(GROUPS, 128).T
    wo = np.zeros((4, 32, GROUPS, D), np.float32)
    wo[:, :DH] = att["Wo"].reshape(GROUPS, 4, DH, D).transpose(1, 2, 0, 3)
    arrays = {
        "idx0": tok["idx0"].reshape(2, 128, GP).transpose(1, 0, 2),
        "idx1": tok["idx1"].reshape(G1, 2, 8).transpose(2, 1, 0).reshape(1, P1),
        "rowid": np.arange(P1, dtype=np.float32).reshape(P1 // 128, 128).T,
        "idx2": tok["idx2"].reshape(G2, 2, 8).transpose(2, 0, 1).reshape(128, 2),
        "table0": table(1), "table1": table(2), "table2": table(4),
        "ident": np.eye(128, dtype=np.float32),
        "interp": np.concatenate([interpolation(G1, NTOK), interpolation(G2, NTOK)], 1).reshape(2, 128, G1 + G2).transpose(1, 0, 2),
        "W0": tok["W0"],
        "W1T": tok["W1"].T.reshape(2, 8 * F1, EMB).transpose(1, 0, 2),
        "W2T": tok["W2"].T.reshape(GP, F2, EMB).transpose(1, 0, 2),
        "WfT": tok["Wf"].T.reshape(3, EMB, D).transpose(1, 0, 2),
        "b0": tok["b0"].reshape(EMB, 1), "b1": tok["b1"].reshape(EMB, 1), "b2": tok["b2"].reshape(EMB, 1),
        "bf": tok["bf"].reshape(1, D),
        "txt": i["txt"],
        "wqk0": wqk[:DC], "wqk1": wqk[DC:], "wv0": wv[:DC], "wv1": wv[DC:], "bqk": bqk,
        "wo": wo.reshape(128, GROUPS, D),
        "bvrow": rows(att["bv"]), "borow": rows(att["bo"]), "b2row": rows(ffn["b2"]),
        "aa1row": rows(ffn["alpha_a1"]), "aa2row": rows(ffn["alpha_a2"]),
        "w1f0": ffn["w1"].T[:DC], "w1f1": ffn["w1"].T[DC:],
        "w2f": ffn["w2"].T.reshape(MH, 128, D).transpose(1, 0, 2),
        "aw1row": rows(ffn["alpha_w1"]), "aw2row": rows(ffn["alpha_w2"]),
        "aw1col": ffn["alpha_w1"].reshape(MH, 128).T, "b1col": ffn["b1"].reshape(MH, 128).T,
    }
    arrays = {k: np.ascontiguousarray(v) for k, v in arrays.items()}
    nc = bacc.Bacc("TRN2", target_bir_lowering=False, num_devices=1)
    given = {k: nc.dram_tensor(f"in_{k}", v.shape, mybir.dt.from_np(v.dtype), kind="ExternalInput").ap() for k, v in arrays.items()}
    out = nc.dram_tensor("out", (B, S, D), F32, kind="ExternalOutput").ap()
    build(nc, given, out.rearrange("b (t p) d -> b p t d", p=128))
    r = run_bass_kernel_spmd(nc, [{f"in_{k}": v for k, v in arrays.items()}], core_ids=[0])
    return r.results[0]["out"]
```
